# Optimizing a Trainium2 kernel written in Bass

```python
import numpy as np
import jax
import jax.numpy as jnp

def _softmax(x, axis=-1):
    return jax.nn.softmax(x, axis=axis)

def _gelu(x):
    return jax.nn.gelu(x, approximate=True)

def _silu(x):
    return jax.nn.silu(x)

def _sigmoid(x):
    return jax.nn.sigmoid(x)

def _layernorm(x, axis=-1, eps=1e-05):
    m = jnp.mean(x, axis=axis, keepdims=True)
    v = jnp.var(x, axis=axis, keepdims=True)
    return (x - m) / jnp.sqrt(v + eps)

def _scatter_add(tgt, idx, src, axis=0):
    return tgt.at[idx].add(src)

def _segment_sum(src, seg, n):
    return jax.ops.segment_sum(src, seg, n)
kernel_name = 'mk_adj_preln_d2_adj_r2_fa40a3'

def setup_inputs(seed: int=0):
    np.random.seed(seed)
    _w = jnp.asarray

    def _rec_inputs():
        import jax
        import jax.numpy as jnp
        _gk = jax.random.key(seed)
        x = -0.0005207 + 1.001 * jax.random.normal(jax.random.fold_in(_gk, 1), (4096, 128), jnp.float32)
        _a = jax.random.bernoulli(jax.random.fold_in(_gk, 2), 0.000488281, (4096, 4096))
        _a = jnp.logical_or(_a, jnp.eye(4096, dtype=bool))
        _af = _a.astype(jnp.float32)
        _af = _af * jax.random.uniform(jax.random.fold_in(_gk, 3), (4096, 4096), jnp.float32, 0.05, 1)
        adj = _af
        return (x, adj)
    x, adj = _rec_inputs()

    def _L0_gnn_setup():
        import jax, jax.numpy as jnp
        import numpy as np
        N = 4096
        D = 128
        L = 3

        def _cxin_conv(x, a, eps, W, b):
            ax = a @ x
            h = ax + (1.0 + eps[0]) * ax
            for i in range(L):
                h = jax.nn.relu(h @ W[i].T + b[i])
            return h
        key = jax.random.key(seed)
        ks = jax.random.split(key, 8)
        s = 1.0 / np.sqrt(D)
        return {'x1': jax.random.normal(ks[0], (N, D), jnp.float32), 'x2': jax.random.normal(ks[1], (N, D), jnp.float32), 'G1': jax.random.uniform(ks[2], (N, N), jnp.float32), 'G2': jax.random.uniform(ks[3], (N, N), jnp.float32), 'eps1': jnp.zeros((1,), jnp.float32), 'eps2': jnp.zeros((1,), jnp.float32), 'W1': jax.random.normal(ks[4], (L, D, D), jnp.float32) * s, 'b1': jnp.zeros((L, D), jnp.float32), 'W2': jax.random.normal(ks[5], (L, D, D), jnp.float32) * s, 'b2': jnp.zeros((L, D), jnp.float32), 'Wm': jax.random.normal(ks[6], (D, 2 * D), jnp.float32) * (1.0 / np.sqrt(2 * D)), 'bm': jnp.zeros((D,), jnp.float32)}
    _L0_gnn_all = _L0_gnn_setup()
    _L0_gnn_in = {k: v for k, v in _L0_gnn_all.items() if k in ('x2', 'eps1', 'eps2', 'W1', 'b1', 'W2', 'b2', 'Wm', 'bm')}
    del _L0_gnn_all

    def _L1_gnn_setup():
        import jax, jax.numpy as jnp
        import numpy as np
        N = 10000
        D = 128
        F = 128
        K = F // 8
        key = jax.random.key(seed)
        k1, k2, k3, k4, k5 = jax.random.split(key, 5)
        h = jax.random.normal(k1, (N, D), dtype=jnp.float32)
        adj = jax.random.uniform(k2, (N, N), dtype=jnp.float32)
        W1 = jax.random.normal(k3, (D, K), dtype=jnp.float32) * 0.05
        W2 = jax.random.normal(k4, (K, D, F), dtype=jnp.float32) * 0.05
        b = jax.random.normal(k5, (K, F), dtype=jnp.float32) * 0.05
        return {'h': h, 'adj': adj, 'W1': W1, 'W2': W2, 'b': b}
    _L1_gnn_all = _L1_gnn_setup()
    _L1_gnn_in = {k: v for k, v in _L1_gnn_all.items() if k in ('W1', 'W2', 'b')}
    del _L1_gnn_all
    return {'x': x, 'adj': adj, 'L0_gnn_x2': _L0_gnn_in['x2'], 'L0_gnn_eps1': _L0_gnn_in['eps1'], 'L0_gnn_eps2': _L0_gnn_in['eps2'], 'L0_gnn_W1': _L0_gnn_in['W1'], 'L0_gnn_b1': _L0_gnn_in['b1'], 'L0_gnn_W2': _L0_gnn_in['W2'], 'L0_gnn_b2': _L0_gnn_in['b2'], 'L0_gnn_Wm': _L0_gnn_in['Wm'], 'L0_gnn_bm': _L0_gnn_in['bm'], 'L1_gnn_W1': _L1_gnn_in['W1'], 'L1_gnn_W2': _L1_gnn_in['W2'], 'L1_gnn_b': _L1_gnn_in['b']}

def reference(x, adj, L0_gnn_x2, L0_gnn_eps1, L0_gnn_eps2, L0_gnn_W1, L0_gnn_b1, L0_gnn_W2, L0_gnn_b2, L0_gnn_Wm, L0_gnn_bm, L1_gnn_W1, L1_gnn_W2, L1_gnn_b):
    import jax
    import jax.numpy as jnp

    def _L0_gnn_ref(x1, x2, G1, G2, eps1, eps2, W1, b1, W2, b2, Wm, bm):
        import jax, jax.numpy as jnp
        import numpy as np
        N = 4096
        D = 128
        L = 3

        def _cxin_conv(x, a, eps, W, b):
            ax = a @ x
            h = ax + (1.0 + eps[0]) * ax
            for i in range(L):
                h = jax.nn.relu(h @ W[i].T + b[i])
            return h
        out1 = _cxin_conv(x1, G1, eps1, W1, b1)
        out2 = _cxin_conv(x2, G2, eps2, W2, b2)
        merged = jnp.concatenate((out1, out2), axis=1)
        return merged @ Wm.T + bm

    def _L1_gnn_ref(h, adj, W1, W2, b):
        import jax, jax.numpy as jnp
        import numpy as np
        N = 10000
        D = 128
        F = 128
        K = F // 8
        node = h @ W1
        hw = jnp.einsum('nc,kcf->nkf', h, W2)
        x = jnp.einsum('nk,nkf->nf', node, hw)
        x = adj @ x
        x = x + node @ b
        return jax.nn.relu(x)
    h = jnp.maximum(_layernorm(x, axis=-1), 0.0)
    x = x + _L0_gnn_ref(h, L0_gnn_x2, adj, adj, L0_gnn_eps1, L0_gnn_eps2, L0_gnn_W1, L0_gnn_b1, L0_gnn_W2, L0_gnn_b2, L0_gnn_Wm, L0_gnn_bm)
    h = jnp.maximum(_layernorm(x, axis=-1), 0.0)
    x = x + _L1_gnn_ref(h, adj, L1_gnn_W1, L1_gnn_W2, L1_gnn_b)
    return x

_drawn_inputs = setup_inputs


def setup_inputs(seed=0):
    import zlib

    import numpy as np

    out = dict(_drawn_inputs(seed))
    spreads = {'L0_gnn_b1': (0.0, 0.1), 'L0_gnn_b2': (0.0, 0.1), 'L0_gnn_bm': (0.0, 0.1)}
    factors = {}
    for name, (base, spread) in spreads.items():
        noise = np.random.default_rng([zlib.crc32(name.encode()), seed]).standard_normal(out[name].shape)
        drawn = base * np.exp(spread * noise) if base else spread * noise
        out[name] = jnp.asarray(drawn.astype(out[name].dtype))
    for name, factor in factors.items():
        out[name] = (out[name] * factor).astype(out[name].dtype)
    return out
```

```python
from contextlib import ExitStack

import concourse.bass as bass
from concourse import mybir

F32 = mybir.dt.float32
F32R = mybir.dt.float32r
ALU = mybir.AluOpType
ACT = mybir.ActivationFunctionType
AX_X = mybir.AxisListType.X

P = 128
D = 128
BLOCK = 512
TILES = BLOCK // P
PER_CHUNK = 2
RING = 4
LAYERS = 3
LN_EPS = 1e-5
LN_STEPS = 11


def two_layer_graph_kernel(nc, x, adj_t, x2, eps1, eps2, mlp1_w, mlp1_b, mlp2_w, mlp2_b, merge_w, merge_b,
                           node_w, node_w_t, pair_w, node_bias, out):
    N = x.shape[0]
    NODE_TILES = N // P
    BLOCKS = N // BLOCK
    CHUNKS = NODE_TILES // PER_CHUNK
    K = node_w.shape[1]
    QK = BLOCK // D
    QUARTERS = K // QK
    AUX = D + K
    PAIRS = BLOCKS // 2
    LAG = 3

    x_tiles = x.rearrange("(t p) d -> p t d", p=P)
    x2_tiles = x2.rearrange("(t p) d -> p t d", p=P)
    out_tiles = out.rearrange("(b t p) d -> b p t d", p=P, t=TILES)

    with ExitStack() as ctx:
        def sb(name, shape, dt=F32):
            return ctx.enter_context(nc.sbuf_tensor(name, shape, dt))

        def sem(name):
            return ctx.enter_context(nc.semaphore(name))

        adj_raw = sb("adj_raw", [P, RING, PER_CHUNK * BLOCK])
        adj_hi = sb("adj_hi", [P, RING, PER_CHUNK * BLOCK], F32R)
        adj_lo = sb("adj_lo", [P, RING, PER_CHUNK * BLOCK], F32R)
        h_hi = sb("h_hi", [P, NODE_TILES, D], F32R)
        h_lo = sb("h_lo", [P, NODE_TILES, D], F32R)
        x2_hi = sb("x2_hi", [P, NODE_TILES, D], F32R)
        x2_lo = sb("x2_lo", [P, NODE_TILES, D], F32R)
        y_hi, y_lo = h_hi, h_lo
        y = sb("y", [P, NODE_TILES, D])
        x_res = sb("x_res", [P, NODE_TILES, D])
        node_b = sb("node_b", [P, NODE_TILES, D])
        pair_hi = sb("pair_hi", [P, K * D], F32R)
        pair_lo = sb("pair_lo", [P, K * D], F32R)
        aux_hi = sb("aux_hi", [P, AUX], F32R)
        aux_lo = sb("aux_lo", [P, AUX], F32R)
        w1_f32 = sb("w1_f32", [P, K])
        w1t_f32 = sb("w1t_f32", [K, D])
        nb_f32 = sb("nb_f32", [K, D])
        mlp_w = sb("mlp_w", [P, 2, LAYERS, D])
        mlp_b = sb("mlp_b", [P, 2, LAYERS])
        mrg_w = sb("mrg_w", [P, 2, D])
        bm_all = sb("bm_all", [P, D])
        scale = sb("scale", [P, 2])
        ident = sb("ident", [P, P])
        ln_eps = sb("ln_eps", [P, 1])
        act = [sb("act1", [P, BLOCK]), sb("act2", [P, BLOCK])]
        cen = sb("cen", [P, TILES, D])
        sq = sb("sq", [P, TILES, D])
        normed = sb("normed", [P, TILES, D])
        h2t_hi = sb("h2t_hi", [P, BLOCK], F32R)
        h2t_lo = sb("h2t_lo", [P, BLOCK], F32R)
        node = sb("node", [P, TILES, K])
        prod = sb("prod", [P, QUARTERS, QK, D])
        psums = sb("psums", [P, QK, D])
        stat = sb("stat", [P, 8, TILES])
        row_sum, mean, sq_sum, var, std, rstd, newton = (stat[:, n, :] for n in range(7))
        out_buf = [sq, normed]

        bank = [ctx.enter_context(nc.psum_tensor(f"bank{n}", [P, BLOCK], F32)) for n in range(8)]
        acc_h, acc_x2 = bank[0], bank[1]
        acc_y = [bank[0], bank[1]]
        mlp_acc = [bank[2], bank[3]]
        pair_acc = bank[4:8]
        merged, turned = bank[4], bank[5]
        out_acc = [bank[6], bank[7]]

        raw_full = [sem(f"raw_full{n}") for n in range(RING)]
        hi_ready = sem("hi_ready")
        lo_ready = sem("lo_ready")
        chunk_used = sem("chunk_used")
        x_in = [sem(f"x_in{n}") for n in range(2)]
        x2_in = [sem(f"x2_in{n}") for n in range(2)]
        weights_in = sem("weights_in")
        pair_in = sem("pair_in")
        consts = sem("consts")
        ln_step = sem("ln_step")
        ln_sq = sem("ln_sq")
        ln_std = sem("ln_std")
        h_hi_ready = sem("h_hi_ready")
        h_lo_ready = sem("h_lo_ready")
        res_ready = sem("res_ready")
        x2_hi_ready = sem("x2_hi_ready")
        x2_lo_ready = sem("x2_lo_ready")
        scale_ready = sem("scale_ready")
        w1b_acc = sem("w1b_acc")
        aux_hi_ready = sem("aux_hi_ready")
        aux_lo_ready = sem("aux_lo_ready")
        pair_hi_ready = sem("pair_hi_ready")
        pair_lo_ready = sem("pair_lo_ready")
        acc_h_done = sem("acc_h_done")
        act_ready = [sem("act1_ready"), sem("act2_ready")]
        mlp_done = [sem("mlp1_done"), sem("mlp2_done")]
        merge_done = sem("merge_done")
        x0_kept = sem("x0_kept")
        turn_done = sem("turn_done")
        h2t_hi_ready = sem("h2t_hi_ready")
        h2t_lo_ready = sem("h2t_lo_ready")
        aux_done = sem("aux_done")
        node_ready = sem("node_ready")
        pair_done = sem("pair_done")
        prod_done = sem("prod_done")
        sum_step = sem("sum_step")
        y_hi_ready = sem("y_hi_ready")
        y_lo_ready = sem("y_lo_ready")
        accy_out = sem("accy_out")
        back_done = sem("back_done")
        biased = sem("biased")
        out_ready = sem("out_ready")
        out_stored = [sem(f"out_stored{n}") for n in range(2)]

        SUM_STEPS = QUARTERS + 1
        BANKS = TILES * QUARTERS

        block = ctx.enter_context(nc.Block())

        @block.sync
        def _(sp):
            def load_chunk(blk, source, c, wait):
                if wait:
                    sp.wait_ge(lo_ready, blk * CHUNKS + c - RING + 1)
                sp.dma_start(adj_raw[:, c % RING, :], adj_t[source, c]).then_inc(raw_full[c % RING], 16)

            for c in range(CHUNKS):
                load_chunk(0, 0, c, c >= RING)
            with sp.Fori(0, BLOCKS - 1) as b:
                for c in range(CHUNKS):
                    load_chunk(b + 1, b + 1, c, True)
            for c in range(CHUNKS):
                load_chunk(BLOCKS, 0, c, True)

            def store(b, parity):
                sp.wait_ge(out_ready, b + 2)
                sp.dma_start(out_tiles[b], out_buf[parity][:]).then_inc(out_stored[parity], 16)

            def second_pass_block(b, parity):
                for c in range(CHUNKS):
                    load_chunk(b + BLOCKS, b, c, True)
                    if c == LAG + RING + 3:
                        store(b - 1, 1 - parity)

            second_pass_block(1, 1)
            with sp.Fori(0, PAIRS - 1) as pair:
                second_pass_block(pair * 2 + 2, 0)
                second_pass_block(pair * 2 + 3, 1)
            store(BLOCKS - 1, 1)
            for parity in range(2):
                sp.wait_ge(out_stored[parity], 16 * (PAIRS + 1))

        @block.gpsimd
        def _(pool):
            nc.gpsimd.memset(ln_eps[:], LN_EPS).then_inc(consts, 1)
            nc.gpsimd.memset(ident[:], 0.0).then_inc(consts, 1)
            pool.wait_ge(consts, 2)
            nc.gpsimd.affine_select(out=ident[:], in_=ident[:], compare_op=ALU.not_equal, fill=1.0, base=0,
                                    pattern=[[-1, P]], channel_multiplier=1).then_inc(consts, 1)

            pool.wait_ge(weights_in, 16 * 11)
            for g in range(BLOCKS):
                t = slice(g * TILES, (g + 1) * TILES)
                pool.wait_ge(x2_hi_ready, g + 1)
                nc.gpsimd.tensor_tensor(x2_lo[:, t, :], y[:, t, :], x2_hi[:, t, :].bitcast(F32),
                                        ALU.subtract).then_inc(x2_lo_ready, 1)
                pool.wait_ge(ln_step, LN_STEPS * g + 4)
                bm = bm_all[:].rearrange("p (o d) -> p o d", o=1).to_broadcast([P, TILES, D])
                nc.gpsimd.tensor_tensor(x_res[:, t, :], x_res[:, t, :], bm, ALU.add).then_inc(res_ready, 1)
            for n in range(QUARTERS):
                cols = slice(n * BLOCK, (n + 1) * BLOCK)
                pool.wait_ge(pair_hi_ready, n + 1)
                done = nc.gpsimd.tensor_tensor(pair_lo[:, cols], prod[:, n, :, :].rearrange("p k f -> p (k f)"),
                                               pair_hi[:, cols].bitcast(F32), ALU.subtract)
                done.then_inc(pair_lo_ready, 1)
            nc.gpsimd.memset(psums[:, 0, 0:1], 0.0).then_inc(sum_step, SUM_STEPS)

            def sum_tile(b, j):
                banks = b * BANKS + j * QUARTERS + 1
                steps = (b * TILES + (j + 1)) * SUM_STEPS
                pool.wait_ge(prod_done, banks + 2)
                pool.wait_ge(sum_step, steps)
                nc.gpsimd.tensor_tensor(psums[:], prod[:, 0], prod[:, 1], ALU.add).then_inc(sum_step, 1)
                for q in range(2, QUARTERS):
                    pool.wait_ge(prod_done, banks + q + 1)
                    pool.wait_ge(sum_step, steps + q - 1)
                    nc.gpsimd.tensor_tensor(psums[:], psums[:], prod[:, q], ALU.add).then_inc(sum_step, 1)
                pool.wait_ge(sum_step, steps + QUARTERS - 1)
                nc.gpsimd.tensor_tensor(psums[:, 0:2], psums[:, 0:2], psums[:, 2:4], ALU.add).then_inc(sum_step, 1)
                pool.wait_ge(sum_step, steps + QUARTERS)
                nc.gpsimd.tensor_tensor(y[:, bass.ds(b * TILES + j, 1), :], psums[:, 0:1], psums[:, 1:2],
                                        ALU.add).then_inc(sum_step, 1)

            with pool.Fori(0, BLOCKS) as b:
                pool.wait_ge(ln_step, (b + BLOCKS) * LN_STEPS + 1)
                nc.gpsimd.tensor_copy(x_res[:, bass.ds(b * TILES, TILES), :], normed[:]).then_inc(x0_kept, 1)
                for j in range(TILES):
                    sum_tile(b, j)

        @block.scalar
        def _(sc):
            for half in range(2):
                t = slice(half * NODE_TILES // 2, (half + 1) * NODE_TILES // 2)
                sc.dma_start(x_res[:, t, :], x_tiles[:, t, :]).then_inc(x_in[half], 16)
                sc.dma_start(y[:, t, :], x2_tiles[:, t, :]).then_inc(x2_in[half], 16)
            for br, (w, bias, e) in enumerate(((mlp1_w, mlp1_b, eps1), (mlp2_w, mlp2_b, eps2))):
                sc.dma_start(mlp_w[:, br], w).then_inc(weights_in, 16)
                sc.dma_start(mlp_b[:, br], bias).then_inc(weights_in, 16)
                sc.dma_start(scale[:, br:br + 1], e.rearrange("(o e) -> o e", o=1).to_broadcast([P, 1])).then_inc(weights_in, 16)
            sc.dma_start(mrg_w[:], merge_w).then_inc(weights_in, 16)
            sc.dma_start(bm_all[:], merge_b.rearrange("(o e) -> o e", o=1).to_broadcast([P, D])).then_inc(weights_in, 16)
            sc.dma_start(w1_f32[:], node_w).then_inc(weights_in, 16)
            sc.dma_start(w1t_f32[:], node_w_t).then_inc(weights_in, 16)
            sc.dma_start(nb_f32[:], node_bias).then_inc(weights_in, 16)
            sc.dma_start(prod[:].rearrange("p q k f -> p (q k f)"), pair_w).then_inc(pair_in, 16)

            def adj_hi_part(blk, c, held):
                sc.wait_ge(raw_full[c % RING], (blk * (CHUNKS // RING) + c // RING + 1) * 16)
                if held:
                    sc.wait_ge(chunk_used, blk * CHUNKS + c - RING + 1)
                nc.scalar.activation(adj_hi[:, c % RING, :], adj_raw[:, c % RING, :], ACT.Copy).then_inc(hi_ready, 1)

            def ln_square(g):
                sc.wait_ge(ln_step, g * LN_STEPS + 4)
                nc.scalar.activation(sq[:], cen[:], ACT.Square).then_inc(ln_sq, 1)

            def ln_root(g):
                sc.wait_ge(ln_step, g * LN_STEPS + 6)
                nc.scalar.activation(std, var, ACT.Sqrt).then_inc(ln_std, 1)

            def take_acc(b, br):
                if br == 0:
                    sc.wait_ge(acc_h_done, b + 1)
                else:
                    sc.wait_ge(chunk_used, (b + 1) * CHUNKS)
                nc.scalar.activation(act[br][:], (acc_h, acc_x2)[br][:], ACT.Copy,
                                     scale=scale[:, br:br + 1]).then_inc(act_ready[br], 1)

            def mlp_relu(b, layer):
                for br in range(2):
                    sc.wait_ge(mlp_done[br], b * LAYERS + layer + 1)
                    nc.scalar.activation(act[br][:], mlp_acc[br][:], ACT.Relu,
                                         bias=mlp_b[:, br, layer:layer + 1]).then_inc(act_ready[br], 1)

            def take_turned(b):
                sc.wait_ge(turn_done, b + 1)
                nc.scalar.activation(h2t_hi[:], turned[:], ACT.Copy).then_inc(h2t_hi_ready, 1)

            def take_aux(b):
                for half in range(2):
                    got = mlp_acc[half][:, 0:2 * AUX].rearrange("p (t c) -> p t c", t=2)
                    sc.wait_ge(aux_done, b * 2 + half + 1)
                    nc.scalar.activation(node_b[:, bass.ds(b * TILES + 2 * half, 2), :], got[:, :, 0:D], ACT.Copy)
                    nc.scalar.activation(node[:, 2 * half:2 * half + 2, :], got[:, :, D:AUX],
                                         ACT.Copy).then_inc(node_ready, 1)

            def node_work(b):
                return {LAG - 1: [lambda: take_acc(b, 0), lambda: take_acc(b, 1)],
                        LAG: [lambda: mlp_relu(b, 0)],
                        LAG + 1: [lambda: mlp_relu(b, 1)],
                        LAG + 2: [lambda: mlp_relu(b, 2)],
                        LAG + 4: [lambda: ln_square(b + BLOCKS)],
                        LAG + 5: [lambda: ln_root(b + BLOCKS)],
                        LAG + 7: [lambda: take_turned(b)],
                        LAG + 8: [lambda: take_aux(b)]}

            nc.scalar.wait_ge(consts, 3)
            nc.scalar.activation(std[:, 0:1], ln_eps[:], ACT.Sqrt)

            def first_part(g):
                t = slice(g * TILES, (g + 1) * TILES)
                sc.wait_ge(x2_in[g // (BLOCKS // 2)], 16)
                nc.scalar.activation(x2_hi[:, t, :], y[:, t, :], ACT.Copy).then_inc(x2_hi_ready, 1)
                ln_square(g)
                ln_root(g)
                sc.wait_ge(ln_step, (g + 1) * LN_STEPS)
                nc.scalar.activation(h_hi[:, t, :], normed[:], ACT.Copy).then_inc(h_hi_ready, 1)

            first_part(0)
            for c in range(CHUNKS):
                adj_hi_part(0, c, c >= RING)
                if c % 2 == 1 and c // 2 + 1 < BLOCKS:
                    first_part(c // 2 + 1)
            sc.wait_ge(pair_in, 16)
            for n in range(QUARTERS):
                nc.scalar.activation(pair_hi[:, n * BLOCK:(n + 1) * BLOCK], prod[:, n, :, :].rearrange("p k f -> p (k f)"),
                                     ACT.Copy).then_inc(pair_hi_ready, 1)
            sc.wait_ge(weights_in, 16 * 11)
            nc.scalar.activation(aux_hi[:, D:AUX], w1_f32[:], ACT.Copy).then_inc(aux_hi_ready, 1)
            sc.wait_ge(w1b_acc, 1)
            nc.scalar.activation(aux_hi[:, 0:D], bank[2][:, 0:D], ACT.Copy).then_inc(aux_hi_ready, 1)
            sc.wait_ge(scale_ready, 1)

            with sc.Fori(0, BLOCKS - 1) as b:
                work = node_work(b)
                for c in range(CHUNKS):
                    adj_hi_part(b + 1, c, True)
                    for step in work.get(c, []):
                        step()

            def y_hi_part(g):
                t = slice(g * TILES, (g + 1) * TILES)
                sc.wait_ge(sum_step, (g * TILES + TILES + 1) * SUM_STEPS)
                sc.wait_ge(chunk_used, BLOCKS * CHUNKS)
                nc.scalar.activation(y_hi[:, t, :], y[:, t, :], ACT.Copy).then_inc(y_hi_ready, 1)

            work = node_work(BLOCKS - 1)
            for c in range(CHUNKS):
                adj_hi_part(BLOCKS, c, True)
                if c == LAG - 1:
                    y_hi_part(0)
                for step in work.get(c, []):
                    step()
                if c >= LAG - 1 and c - LAG + 2 < BLOCKS - 1:
                    y_hi_part(c - LAG + 2)

            def take_accy(b, parity):
                sc.wait_ge(chunk_used, (b + BLOCKS + 1) * CHUNKS)
                nc.scalar.activation(act[parity][:], acc_y[parity][:], ACT.Copy).then_inc(accy_out, 1)

            def second_pass_block(b, parity):
                for c in range(CHUNKS):
                    adj_hi_part(b + BLOCKS, c, True)
                    if c == LAG - 1:
                        take_accy(b - 1, 1 - parity)

            y_hi_part(BLOCKS - 1)
            second_pass_block(1, 1)
            with sc.Fori(0, PAIRS - 1) as pair:
                second_pass_block(pair * 2 + 2, 0)
                second_pass_block(pair * 2 + 3, 1)
            take_accy(BLOCKS - 1, 1)

        @block.vector
        def _(ve):
            def adj_lo_part(blk, c, held):
                ve.wait_ge(hi_ready, blk * CHUNKS + c + 1)
                if held:
                    ve.wait_ge(chunk_used, blk * CHUNKS + c - RING + 1)
                nc.vector.tensor_tensor(adj_lo[:, c % RING, :], adj_raw[:, c % RING, :],
                                        adj_hi[:, c % RING, :].bitcast(F32), ALU.subtract).then_inc(lo_ready, 1)

            def over_row(v):
                return v.rearrange("p (t o) -> p t o", o=1).to_broadcast([P, TILES, D])

            def ln_centre(g, rows):
                at = g * LN_STEPS
                ve.wait_ge(ln_step, at + 1)
                nc.vector.tensor_reduce(row_sum, rows, AX_X, ALU.add).then_inc(ln_step, 1)
                ve.wait_ge(ln_step, at + 2)
                nc.vector.tensor_scalar(mean, row_sum, 1.0 / D, None, ALU.mult).then_inc(ln_step, 1)
                ve.wait_ge(ln_step, at + 3)
                nc.vector.tensor_tensor(cen[:], rows, over_row(mean), ALU.subtract).then_inc(ln_step, 1)

            def ln_variance(g):
                at = g * LN_STEPS + 4
                ve.wait_ge(ln_sq, g + 1)
                nc.vector.tensor_reduce(sq_sum, sq[:], AX_X, ALU.add).then_inc(ln_step, 1)
                ve.wait_ge(ln_step, at + 1)
                nc.vector.tensor_scalar(var, sq_sum, 1.0 / D, LN_EPS, ALU.mult, ALU.add).then_inc(ln_step, 1)

            def ln_scale(g):
                at = g * LN_STEPS + 6
                ve.wait_ge(ln_std, g + 1)
                nc.vector.reciprocal(rstd, std).then_inc(ln_step, 1)
                ve.wait_ge(ln_step, at + 1)
                nc.vector.tensor_tensor(newton, rstd, rstd, ALU.mult).then_inc(ln_step, 1)
                ve.wait_ge(ln_step, at + 2)
                nc.vector.scalar_tensor_tensor(newton, newton, -0.5, var, ALU.mult, ALU.mult).then_inc(ln_step, 1)
                ve.wait_ge(ln_step, at + 3)
                nc.vector.scalar_tensor_tensor(rstd, newton, 1.5, rstd, ALU.add, ALU.mult).then_inc(ln_step, 1)
                ve.wait_ge(ln_step, at + 4)
                nc.vector.scalar_tensor_tensor(normed[:], cen[:], 0.0, over_row(rstd), ALU.max,
                                               ALU.mult).then_inc(ln_step, 1)

            def add_residual(b):
                t = bass.ds(b * TILES, TILES)
                ve.wait_ge(merge_done, b + 1)
                nc.vector.tensor_tensor(normed[:], merged[:].rearrange("p (t d) -> p t d", t=TILES),
                                        x_res[:, t, :], ALU.add).then_inc(ln_step, 1)
                ln_centre(b + BLOCKS, normed[:])

            def h2t_lo_part(b):
                ve.wait_ge(h2t_hi_ready, b + 1)
                nc.vector.tensor_tensor(h2t_lo[:], turned[:], h2t_hi[:].bitcast(F32),
                                        ALU.subtract).then_inc(h2t_lo_ready, 1)

            def weigh(b, n):
                j, q = n // QUARTERS, n % QUARTERS
                ve.wait_ge(pair_done, b * BANKS + n + 1)
                ve.wait_ge(node_ready, b * 2 + j // 2 + 1)
                ve.wait_ge(sum_step, (b * TILES + j) * SUM_STEPS + max(q, 1))
                coef = node[:, j, q * QK:(q + 1) * QK].rearrange("p (k o) -> p k o", o=1).to_broadcast([P, QK, D])
                nc.vector.tensor_tensor(prod[:, q], pair_acc[q][:].rearrange("p (k f) -> p k f", k=QK), coef,
                                        ALU.mult).then_inc(prod_done, 1)

            def node_work(b):
                work = {LAG + 3: [lambda: add_residual(b)],
                        LAG + 4: [lambda: ln_variance(b + BLOCKS)],
                        LAG + 5: [lambda: ve.wait_ge(x0_kept, b + 1), lambda: ln_scale(b + BLOCKS)],
                        LAG + 7: [lambda: h2t_lo_part(b)]}
                for n in range(BANKS):
                    at = min(LAG + 8 + n // 3, CHUNKS - 1)
                    work.setdefault(at, []).append(lambda n=n: weigh(b, n))
                return work

            nc.vector.memset(newton, 0.0).then_inc(prod_done, 1)
            nc.vector.memset(mean, 0.0).then_inc(out_ready, 1)
            for parity in range(2):
                nc.vector.memset(stat[:, 7, parity:parity + 1], 0.0).then_inc(out_stored[parity], 16)

            def first_part(g):
                t = slice(g * TILES, (g + 1) * TILES)
                ve.wait_ge(x_in[g // (BLOCKS // 2)], 16)
                if g > 0:
                    ve.wait_ge(h_hi_ready, g)
                nc.vector.memset(stat[:, 7, 2:3], 0.0).then_inc(ln_step, 1)
                ln_centre(g, x_res[:, t, :])
                ln_variance(g)
                ln_scale(g)
                ve.wait_ge(h_hi_ready, g + 1)
                nc.vector.tensor_tensor(h_lo[:, t, :], normed[:], h_hi[:, t, :].bitcast(F32),
                                        ALU.subtract).then_inc(h_lo_ready, 1)

            first_part(0)
            for c in range(CHUNKS):
                adj_lo_part(0, c, c >= RING)
                if c % 2 == 1 and c // 2 + 1 < BLOCKS:
                    first_part(c // 2 + 1)
            ve.wait_ge(weights_in, 16 * 11)
            nc.vector.tensor_scalar(scale[:], scale[:], 2.0, None, ALU.add).then_inc(scale_ready, 1)
            ve.wait_ge(aux_hi_ready, 2)
            nc.vector.tensor_tensor(aux_lo[:, D:AUX], w1_f32[:], aux_hi[:, D:AUX].bitcast(F32), ALU.subtract)
            nc.vector.tensor_tensor(aux_lo[:, 0:D], bank[2][:, 0:D], aux_hi[:, 0:D].bitcast(F32),
                                    ALU.subtract).then_inc(aux_lo_ready, 1)
            ve.wait_ge(res_ready, BLOCKS)
            ve.wait_ge(pair_lo_ready, QUARTERS)

            with ve.Fori(0, BLOCKS - 1) as b:
                work = node_work(b)
                for c in range(CHUNKS):
                    adj_lo_part(b + 1, c, True)
                    for step in work.get(c, []):
                        step()

            def y_lo_part(g):
                t = slice(g * TILES, (g + 1) * TILES)
                ve.wait_ge(y_hi_ready, g + 1)
                nc.vector.tensor_tensor(y_lo[:, t, :], y[:, t, :], y_hi[:, t, :].bitcast(F32),
                                        ALU.subtract).then_inc(y_lo_ready, 1)

            work = node_work(BLOCKS - 1)
            for c in range(CHUNKS):
                adj_lo_part(BLOCKS, c, True)
                if c == LAG - 1:
                    y_lo_part(0)
                if c >= LAG - 1 and c - LAG + 2 < BLOCKS - 1:
                    y_lo_part(c - LAG + 2)
                for step in work.get(c, []):
                    step()
            y_lo_part(BLOCKS - 1)

            def finish(b, parity):
                t = bass.ds(b * TILES, TILES)
                ve.wait_ge(back_done, b + 1)
                nc.vector.tensor_tensor(cen[:], out_acc[parity][:].rearrange("p (t d) -> p t d", t=TILES),
                                        node_b[:, t, :], ALU.add).then_inc(biased, 1)
                ve.wait_ge(biased, b + 1)
                ve.wait_ge(out_stored[parity], (b - parity) * 8 + 16)
                nc.vector.scalar_tensor_tensor(out_buf[parity][:], cen[:], 0.0, x_res[:, t, :], ALU.max,
                                               ALU.add).then_inc(out_ready, 1)

            def second_pass_block(b, parity):
                for c in range(CHUNKS):
                    adj_lo_part(b + BLOCKS, c, True)
                    if c == LAG + 2:
                        finish(b - 1, 1 - parity)

            second_pass_block(1, 1)
            with ve.Fori(0, PAIRS - 1) as pair:
                second_pass_block(pair * 2 + 2, 0)
                second_pass_block(pair * 2 + 3, 1)
            finish(BLOCKS - 1, 1)

        @block.tensor
        def _(pe):
            def exact(acc, hi, lo, right_hi, right_lo, start, stop):
                nc.tensor.matmul(acc, hi, right_hi, start=start, stop=False)
                nc.tensor.matmul(acc, hi, right_lo, start=False, stop=False)
                return nc.tensor.matmul(acc, lo, right_hi, start=False, stop=stop)

            def times_adj(acc, hi, lo, c):
                for n in range(PER_CHUNK):
                    k = c * PER_CHUNK + n
                    cols = slice(n * BLOCK, (n + 1) * BLOCK)
                    done = exact(acc[:], hi[:, k, :], lo[:, k, :], adj_hi[:, c % RING, cols],
                                 adj_lo[:, c % RING, cols], start=(k == 0), stop=(k == NODE_TILES - 1))
                return done

            def first_pass_chunk(blk, c, before=None):
                last = c == CHUNKS - 1
                pe.wait_ge(lo_ready, blk * CHUNKS + c + 1)
                if c == 0 and before is not None:
                    pe.wait_ge(act_ready[0], before * (LAYERS + 1) + 1)
                done = times_adj(acc_h, h_hi, h_lo, c)
                if last:
                    done.then_inc(acc_h_done, 1)
                if c == 0 and before is not None:
                    pe.wait_ge(act_ready[1], before * (LAYERS + 1) + 1)
                done = times_adj(acc_x2, x2_hi, x2_lo, c)
                done.then_inc(chunk_used, 1)

            def mlp_layer(b, layer):
                for br in range(2):
                    pe.wait_ge(act_ready[br], b * (LAYERS + 1) + layer + 1)
                    nc.tensor.matmul(mlp_acc[br][:], mlp_w[:, br, layer, :], act[br][:], start=True,
                                     stop=True).then_inc(mlp_done[br], 1)

            def merge(b):
                for br in range(2):
                    pe.wait_ge(act_ready[br], (b + 1) * (LAYERS + 1))
                pe.wait_ge(prod_done, b * BANKS + 1)
                for j in range(TILES):
                    cols = slice(j * P, (j + 1) * P)
                    for br in range(2):
                        done = nc.tensor.matmul(merged[:, cols], act[br][:, cols], mrg_w[:, br, :],
                                                start=(br == 0), stop=(br == 1))
                done.then_inc(merge_done, 1)

            def turn(b):
                pe.wait_ge(ln_step, (b + BLOCKS + 1) * LN_STEPS)
                for j in range(TILES):
                    done = nc.tensor.transpose(turned[:, j * P:(j + 1) * P], normed[:, j, :], ident[:])
                done.then_inc(turn_done, 1)

            def aux(b):
                pe.wait_ge(h2t_lo_ready, b + 1)
                for j in range(TILES):
                    at = (j % 2) * AUX
                    cols = slice(j * P, (j + 1) * P)
                    done = exact(mlp_acc[j // 2][:, at:at + AUX], h2t_hi[:, cols], h2t_lo[:, cols], aux_hi[:],
                                 aux_lo[:], start=True, stop=True)
                    if j % 2 == 1:
                        done.then_inc(aux_done, 1)

            def pair_bank(b, n):
                j, q = n // QUARTERS, n % QUARTERS
                cols, basis = slice(j * P, (j + 1) * P), slice(q * BLOCK, (q + 1) * BLOCK)
                if n >= QUARTERS:
                    pe.wait_ge(prod_done, b * BANKS + n - QUARTERS + 2)
                exact(pair_acc[q][:], h2t_hi[:, cols], h2t_lo[:, cols], pair_hi[:, basis], pair_lo[:, basis],
                      start=True, stop=True).then_inc(pair_done, 1)

            def node_work(b):
                work = {0: [lambda: mlp_layer(b, 0)],
                        1: [lambda: mlp_layer(b, 1)],
                        2: [lambda: mlp_layer(b, 2)],
                        3: [lambda: merge(b)],
                        6: [lambda: turn(b)],
                        7: [lambda: aux(b)]}
                for n in range(BANKS):
                    work.setdefault(min(8 + n // 3, CHUNKS - 1), []).append(lambda n=n: pair_bank(b, n))
                return work

            pe.wait_ge(weights_in, 16 * 11)
            nc.tensor.matmul(bank[2][:, 0:D], w1t_f32[:], nb_f32[:], start=True, stop=True).then_inc(w1b_acc, 1)
            for c in range(CHUNKS):
                if c % 2 == 0:
                    pe.wait_ge(h_lo_ready, c // 2 + 1)
                    pe.wait_ge(x2_lo_ready, c // 2 + 1)
                first_pass_chunk(0, c)
            pe.wait_ge(aux_lo_ready, 1)
            pe.wait_ge(pair_lo_ready, QUARTERS)
            with pe.Fori(0, BLOCKS - 1) as b:
                work = node_work(b)
                for c in range(CHUNKS):
                    first_pass_chunk(b + 1, c, before=b)
                    for step in work.get(c, []):
                        step()

            def second_pass_chunk(b, c, parity):
                pe.wait_ge(lo_ready, (b + BLOCKS) * CHUNKS + c + 1)
                done = times_adj(acc_y[parity], y_hi, y_lo, c)
                done.then_inc(chunk_used, 1)

            work = node_work(BLOCKS - 1)
            for c in range(CHUNKS):
                if c % 2 == 0:
                    pe.wait_ge(y_lo_ready, c // 2 + 1)
                if c == 0:
                    pe.wait_ge(act_ready[0], (BLOCKS - 1) * (LAYERS + 1) + 1)
                second_pass_chunk(0, c, 0)
                for step in work.get(c, []):
                    step()

            def turn_back(b, parity):
                pe.wait_ge(accy_out, b + 1)
                pe.wait_ge(out_ready, b - parity + 1)
                for j in range(TILES):
                    cols = slice(j * P, (j + 1) * P)
                    done = nc.tensor.transpose(out_acc[parity][:, cols], act[parity][:, cols], ident[:])
                done.then_inc(back_done, 1)

            def second_pass_block(b, parity):
                for c in range(CHUNKS):
                    second_pass_chunk(b, c, parity)
                    if c == 1:
                        turn_back(b - 1, 1 - parity)

            second_pass_block(1, 1)
            with pe.Fori(0, PAIRS - 1) as pair:
                second_pass_block(pair * 2 + 2, 0)
                second_pass_block(pair * 2 + 3, 1)
            turn_back(BLOCKS - 1, 1)


def kernel(**inputs):
    import numpy as np
    import concourse.bacc as bacc
    from concourse.bass_utils import run_bass_kernel_spmd

    def plain(a):
        return np.ascontiguousarray(a)

    adj = np.asarray(inputs["adj"])
    n = adj.shape[0]
    blocks, chunks = n // BLOCK, n // (P * PER_CHUNK)
    adj_t = adj.reshape(blocks, BLOCK, chunks, PER_CHUNK, P).transpose(0, 2, 4, 3, 1)
    arrays = {
        "x": plain(inputs["x"]),
        "adj_t": plain(adj_t).reshape(blocks, chunks, P, PER_CHUNK * BLOCK),
        "x2": plain(inputs["L0_gnn_x2"]),
        "eps1": plain(inputs["L0_gnn_eps1"]),
        "eps2": plain(inputs["L0_gnn_eps2"]),
        "mlp1_w": plain(np.asarray(inputs["L0_gnn_W1"]).transpose(2, 0, 1)),
        "mlp1_b": plain(np.asarray(inputs["L0_gnn_b1"]).T),
        "mlp2_w": plain(np.asarray(inputs["L0_gnn_W2"]).transpose(2, 0, 1)),
        "mlp2_b": plain(np.asarray(inputs["L0_gnn_b2"]).T),
        "merge_w": plain(np.asarray(inputs["L0_gnn_Wm"]).reshape(D, 2, D).transpose(2, 1, 0)),
        "merge_b": plain(inputs["L0_gnn_bm"]),
        "node_w": plain(inputs["L1_gnn_W1"]),
        "node_w_t": plain(np.asarray(inputs["L1_gnn_W1"]).T),
        "pair_w": plain(np.asarray(inputs["L1_gnn_W2"]).transpose(1, 0, 2)).reshape(D, -1),
        "node_bias": plain(inputs["L1_gnn_b"]),
    }
    nc = bacc.Bacc("TRN2", target_bir_lowering=False, num_devices=1)
    args = [nc.dram_tensor(name, a.shape, mybir.dt.from_np(a.dtype), kind="ExternalInput").ap()
            for name, a in arrays.items()]
    out = nc.dram_tensor("out", (n, D), F32, kind="ExternalOutput").ap()
    two_layer_graph_kernel(nc, *args, out)
    result = run_bass_kernel_spmd(nc, [arrays], core_ids=[0])
    return result.results[0]["out"]
```

```python
from contextlib import ExitStack

import concourse.bass as bass
from concourse import mybir

F32 = mybir.dt.float32
F32R = mybir.dt.float32r
ALU = mybir.AluOpType
ACT = mybir.ActivationFunctionType

P = 128
D = 128
BLOCK = 512
TILES = BLOCK // P
PER_CHUNK = 2
RAW_RING = 8
RING = 4
LAG = 3
LAYERS = 3
BRANCHES = 2
LN_EPS = 1e-5
LN_STEPS = 9

FIRST_PASS = {"mlp": (1, 2, 3), "merge": 5, "turn": 8, "aux": 10, "pair": lambda n: 11 + n // 4}
SECOND_PASS = {"mlp": (2, 4, 6), "merge": 8, "turn": 12, "aux": 13, "pair": lambda n: 14 + n // 2}


def plan(steps):
    by_chunk = {}
    for chunk, step in steps:
        by_chunk.setdefault(chunk, []).append(step)
    return by_chunk


def two_layer_graph_kernel(nc, x, adj_t, x2, square_w, small_w, basis_w, row_w, pair_w, out):
    N = x.shape[0]
    NODE_TILES = N // P
    BLOCKS = N // BLOCK
    CHUNKS = NODE_TILES // PER_CHUNK
    K = basis_w.shape[0]
    QK = BLOCK // D
    QUARTERS = K // QK
    BANKS = TILES * QUARTERS
    AUX = D + K
    PAIRS = BLOCKS // 2
    MERGE = BRANCHES * LAYERS * D
    SUM_STEPS = QUARTERS + 1

    LATE = CHUNKS - BLOCK // P // PER_CHUNK
    opening = ([(0, c) for c in range(LATE)] + [(1, c) for c in range(LATE)]
               + [(0, c) for c in range(LATE, CHUNKS)] + [(1, c) for c in range(LATE, CHUNKS)])
    END_OF_0 = opening.index((0, CHUNKS - 1))
    kept_at = list(range(0, 2 * BLOCKS - 2, 2)) + [2 * LATE]
    y_parts_at = [0, 1] + [2 * g - 1 for g in range(2, BLOCKS - 1)] + [2 * LATE - 1]

    x_tiles = x.rearrange("(t p) d -> p t d", p=P)
    x2_tiles = x2.rearrange("(t p) d -> p t d", p=P)
    out_tiles = out.rearrange("(b t p) d -> b p t d", p=P, t=TILES)
    x0_dram = nc.dram_tensor("x0_kept", (P, NODE_TILES, D), F32, kind="Internal").ap()
    node_b_dram = nc.dram_tensor("node_b_kept", (P, NODE_TILES, D), F32, kind="Internal").ap()

    BATCHES = (range(0, 2), range(2, 4), range(4, BLOCKS))
    BATCH_OF = [n for n, groups in enumerate(BATCHES) for _ in groups]

    def batch_tiles(n):
        return slice(BATCHES[n][0] * TILES, (BATCHES[n][-1] + 1) * TILES)

    def tiles_of(g):
        return slice(g * TILES, (g + 1) * TILES)

    with ExitStack() as ctx:
        def sb(name, shape, dt=F32, within=ctx):
            return within.enter_context(nc.sbuf_tensor(name, shape, dt))

        def sem(name):
            return ctx.enter_context(nc.semaphore(name))

        adj_raw = sb("adj_raw", [P, RAW_RING, PER_CHUNK * BLOCK])
        adj_hi = sb("adj_hi", [P, RING, PER_CHUNK * BLOCK], F32R)
        adj_lo = sb("adj_lo", [P, RING, PER_CHUNK * BLOCK], F32R)
        h_hi = sb("h_hi", [P, NODE_TILES, D], F32R)
        h_lo = sb("h_lo", [P, NODE_TILES, D], F32R)
        y_hi, y_lo = h_hi, h_lo
        y = sb("y", [P, NODE_TILES, D])
        pair_hi = sb("pair_hi", [P, K * D], F32R)
        pair_lo = sb("pair_lo", [P, K * D], F32R)
        aux_hi = sb("aux_hi", [P, AUX], F32R)
        aux_lo = sb("aux_lo", [P, AUX], F32R)
        square_hi = sb("square_hi", [P, MERGE + BRANCHES * D], F32R)
        square_lo = sb("square_lo", [P, MERGE + BRANCHES * D], F32R)
        small = sb("small", [P, K + BRANCHES * LAYERS])
        basis = sb("basis", [K, D + P])
        rows = sb("rows", [P, D + BRANCHES])
        ident = sb("ident", [P, P])
        ln_eps = sb("ln_eps", [P, 1])
        act_f32 = sb("act_f32", [P, BRANCHES, BLOCK])
        act_hi = sb("act_hi", [P, BRANCHES, BLOCK], F32R)
        act_lo = sb("act_lo", [P, BRANCHES, BLOCK], F32R)
        x0_new = sb("x0_new", [P, TILES, D])
        normed = sb("normed", [P, TILES, D])
        node_b_new = sb("node_b_new", [P, TILES, D])
        h2t_hi = sb("h2t_hi", [P, BLOCK], F32R)
        h2t_lo = sb("h2t_lo", [P, BLOCK], F32R)
        node = sb("node", [P, TILES, K])
        prod = sb("prod", [P, QUARTERS, QK, D])
        psums = sb("psums", [P, QK, D])
        halves = sb("halves", [P, NODE_TILES, 6])
        stat = sb("stat", [P, 8, NODE_TILES])
        var, std, rstd, newton, mean, mean_gap, squares, spare = (stat[:, n, :] for n in range(8))
        with ExitStack() as first_pass:
            x2_hi = sb("x2_hi", [P, NODE_TILES, D], F32R, first_pass)
            x2_lo = sb("x2_lo", [P, NODE_TILES, D], F32R, first_pass)
        x0 = sb("x0", [P, NODE_TILES, D])
        node_b = sb("node_b", [P, NODE_TILES, D])
        biased_y = node_b_new
        out_buf = [x0_new, normed]
        x2_raw = prod[:].rearrange("p q k f -> p q (k f)")

        bank = [ctx.enter_context(nc.psum_tensor(f"bank{n}", [P, BLOCK], F32)) for n in range(8)]
        acc_h, acc_x2 = bank[0], bank[1]
        acc_y = [bank[0], bank[1]]
        mlp_acc = [bank[2], bank[3]]
        pair_acc = bank[4:8]
        merged, turned = bank[4], bank[5]
        out_acc = [bank[6], bank[7]]

        raw_full = [sem(f"raw_full{n}") for n in range(RAW_RING)]
        hi_ready = sem("hi_ready")
        lo_ready = sem("lo_ready")
        chunk_used = sem("chunk_used")
        x_in = [sem(f"x_in{g}") for g in range(BLOCKS)]
        x2_in = [sem(f"x2_in{n}") for n in range(QUARTERS)]
        square_in = sem("square_in")
        small_in = sem("small_in")
        basis_in = sem("basis_in")
        rows_in = sem("rows_in")
        pair_in = sem("pair_in")
        consts = sem("consts")
        ln_step = sem("ln_step")
        ln_root = sem("ln_root")
        normed_ready = sem("normed_ready")
        h_hi_ready = sem("h_hi_ready")
        h_lo_ready = sem("h_lo_ready")
        bm_added = sem("bm_added")
        x2_hi_ready = sem("x2_hi_ready")
        x2_lo_ready = sem("x2_lo_ready")
        scale_ready = sem("scale_ready")
        w1b_done = sem("w1b_done")
        square_hi_ready = sem("square_hi_ready")
        square_lo_ready = sem("square_lo_ready")
        aux_hi_ready = sem("aux_hi_ready")
        aux_lo_ready = sem("aux_lo_ready")
        pair_hi_ready = sem("pair_hi_ready")
        pair_lo_ready = sem("pair_lo_ready")
        acc_h_done = sem("acc_h_done")
        act_f32_ready = [sem(f"act{n}_f32_ready") for n in range(BRANCHES)]
        act_hi_ready = [sem(f"act{n}_hi_ready") for n in range(BRANCHES)]
        act_lo_ready = [sem(f"act{n}_lo_ready") for n in range(BRANCHES)]
        mlp_done = [sem(f"mlp{n}_done") for n in range(BRANCHES)]
        merge_done = sem("merge_done")
        x0_ready = sem("x0_ready")
        x0_stored = sem("x0_stored")
        turn_done = sem("turn_done")
        h2t_hi_ready = sem("h2t_hi_ready")
        h2t_lo_ready = sem("h2t_lo_ready")
        aux_done = sem("aux_done")
        node_ready = sem("node_ready")
        node_b_stored = sem("node_b_stored")
        pair_done = sem("pair_done")
        prod_done = sem("prod_done")
        sum_step = sem("sum_step")
        y_hi_ready = sem("y_hi_ready")
        y_lo_ready = sem("y_lo_ready")
        kept_in = sem("kept_in")
        accy_out = sem("accy_out")
        back_done = sem("back_done")
        biased = sem("biased")
        out_ready = sem("out_ready")
        out_stored = [sem(f"out_stored{n}") for n in range(2)]

        block = ctx.enter_context(nc.Block())

        @block.sync
        def _(sp):
            def load_chunk(sequence, source, c):
                slot = c % RAW_RING
                sp.dma_start(adj_raw[:, slot, :], adj_t[source, c]).then_inc(raw_full[slot], 16)

            def slot_free(blk, c):
                sp.wait_ge(lo_ready, blk * CHUNKS + c - RAW_RING + 1)

            def load_x(g):
                sp.dma_start(y[:, tiles_of(g), :], x_tiles[:, tiles_of(g), :]).then_inc(x_in[g], 16)

            def load_x2(g):
                if g >= QUARTERS:
                    sp.wait_ge(x2_lo_ready, g - QUARTERS + 1)
                slot = g % QUARTERS
                sp.dma_start(x2_raw[:, slot, :].rearrange("p (t d) -> p t d", t=TILES),
                             x2_tiles[:, tiles_of(g), :]).then_inc(x2_in[slot], 16)

            load_x(0)
            load_x(1)
            load_chunk(0, 0, 0)
            load_x2(0)
            load_chunk(0, 0, 1)
            load_chunk(0, 0, 2)
            load_x2(1)
            load_x(2)
            load_x(3)
            load_chunk(0, 0, 3)
            load_chunk(0, 0, 4)
            load_x2(2)
            load_chunk(0, 0, 5)
            load_x2(3)
            for g in range(4, BLOCKS):
                load_x(g)
            for c in range(6, CHUNKS):
                if c >= RAW_RING:
                    slot_free(0, c)
                load_chunk(0, 0, c)
                if c % 2 == 1 and c // 2 + 1 < BLOCKS:
                    load_x2(c // 2 + 1)
            sp.wait_ge(x2_lo_ready, BLOCKS)
            sp.dma_start(prod[:].rearrange("p q k f -> p (q k f)"), pair_w).then_inc(pair_in, 16)
            with sp.Fori(0, BLOCKS - 1) as b:
                for c in range(CHUNKS):
                    slot_free(b + 1, c)
                    load_chunk(b + 1, b + 1, c)

            def load_kept(g):
                tiles = tiles_of(g)
                sp.wait_ge(chunk_used, (BLOCKS - 1) * CHUNKS + (g + 1) * TILES // PER_CHUNK)
                sp.wait_ge(x0_stored, 16 * (g + 1))
                sp.dma_start(x0[:, tiles, :], x0_dram[:, tiles, :]).then_inc(kept_in, 16)
                sp.wait_ge(node_b_stored, 16 * (g + 1))
                sp.dma_start(node_b[:, tiles, :], node_b_dram[:, tiles, :]).then_inc(kept_in, 16)

            for at, (b, c) in enumerate(opening):
                slot_free(BLOCKS, at)
                sp.dma_start(adj_raw[:, at % RAW_RING, :], adj_t[b, c]).then_inc(raw_full[at % RAW_RING], 16)
                if at in kept_at:
                    load_kept(kept_at.index(at))

            def store(b, parity):
                sp.wait_ge(out_ready, b + 2)
                sp.dma_start(out_tiles[b], out_buf[parity][:]).then_inc(out_stored[parity], 16)

            def second_pass_block(b, parity):
                for c in range(CHUNKS):
                    slot_free(b + BLOCKS, c)
                    load_chunk(b + BLOCKS, b, c)
                    if c == CHUNKS - 4:
                        store(b - 2, parity)

            with sp.Fori(0, PAIRS - 1) as pair:
                second_pass_block(pair * 2 + 2, 0)
                second_pass_block(pair * 2 + 3, 1)
            store(BLOCKS - 2, 0)
            store(BLOCKS - 1, 1)
            for parity in range(2):
                sp.wait_ge(out_stored[parity], 16 * (PAIRS + 1))

        @block.gpsimd
        def _(pool):
            nc.gpsimd.memset(ln_eps[:], LN_EPS).then_inc(consts, 1)
            nc.gpsimd.memset(ident[:], 0.0).then_inc(consts, 1)
            pool.wait_ge(consts, 2)
            nc.gpsimd.affine_select(out=ident[:], in_=ident[:], compare_op=ALU.not_equal, fill=1.0, base=0,
                                    pattern=[[-1, P]], channel_multiplier=1).then_inc(consts, 1)

            def add_bm(g):
                pool.wait_ge(normed_ready, g + 1)
                bm = rows[:, 0:D].rearrange("p (o d) -> p o d", o=1).to_broadcast([P, TILES, D])
                nc.gpsimd.tensor_tensor(y[:, tiles_of(g), :], y[:, tiles_of(g), :], bm, ALU.add).then_inc(bm_added, 1)

            for g in range(BLOCKS):
                pool.wait_ge(x2_hi_ready, g + 1)
                slot = x2_raw[:, g % QUARTERS, :].rearrange("p (t d) -> p t d", t=TILES)
                nc.gpsimd.tensor_tensor(x2_lo[:, tiles_of(g), :], slot, x2_hi[:, tiles_of(g), :].bitcast(F32),
                                        ALU.subtract).then_inc(x2_lo_ready, 1)
                if g == 0:
                    pool.dma_start(act_f32[:].rearrange("p b n -> p (b n)"), square_w).then_inc(square_in, 16)
                    pool.dma_start(small[:], small_w).then_inc(small_in, 16)
                    pool.dma_start(basis[:], basis_w).then_inc(basis_in, 16)
                    pool.dma_start(rows[:], row_w.rearrange("(o e) -> o e", o=1).to_broadcast([P, D + BRANCHES])
                                   ).then_inc(rows_in, 16)
                if g == 2:
                    pool.wait_ge(rows_in, 16)
                if g >= 2:
                    add_bm(g - 2)
            add_bm(BLOCKS - 2)
            add_bm(BLOCKS - 1)
            for n in range(QUARTERS):
                cols = slice(n * BLOCK, (n + 1) * BLOCK)
                pool.wait_ge(pair_hi_ready, n + 1)
                nc.gpsimd.tensor_tensor(pair_lo[:, cols], prod[:, n, :, :].rearrange("p k f -> p (k f)"),
                                        pair_hi[:, cols].bitcast(F32), ALU.subtract).then_inc(pair_lo_ready, 1)
            nc.gpsimd.memset(psums[:, 0, 0:1], 0.0).then_inc(sum_step, SUM_STEPS)

            def keep(b):
                pool.wait_ge(x0_ready, b + 1)
                pool.wait_ge(node_ready, b * 2 + 2)
                t = bass.ds(b * TILES, TILES)
                pool.dma_start(x0_dram[:, t, :], x0_new[:]).then_inc(x0_stored, 16)
                pool.dma_start(node_b_dram[:, t, :], node_b_new[:]).then_inc(node_b_stored, 16)

            def sum_tile(b, j):
                banks = b * BANKS + j * QUARTERS + 1
                steps = (b * TILES + (j + 1)) * SUM_STEPS
                pool.wait_ge(prod_done, banks + 2)
                pool.wait_ge(sum_step, steps)
                nc.gpsimd.tensor_tensor(psums[:], prod[:, 0], prod[:, 1], ALU.add).then_inc(sum_step, 1)
                for q in range(2, QUARTERS):
                    pool.wait_ge(prod_done, banks + q + 1)
                    pool.wait_ge(sum_step, steps + q - 1)
                    nc.gpsimd.tensor_tensor(psums[:], psums[:], prod[:, q], ALU.add).then_inc(sum_step, 1)
                pool.wait_ge(sum_step, steps + QUARTERS - 1)
                nc.gpsimd.tensor_tensor(psums[:, 0:2], psums[:, 0:2], psums[:, 2:4], ALU.add).then_inc(sum_step, 1)
                pool.wait_ge(sum_step, steps + QUARTERS)
                nc.gpsimd.tensor_tensor(y[:, bass.ds(b * TILES + j, 1), :], psums[:, 0:1], psums[:, 1:2],
                                        ALU.add).then_inc(sum_step, 1)

            with pool.Fori(0, BLOCKS) as b:
                keep(b)
                for j in range(TILES):
                    if j == TILES - 1:
                        pool.wait_ge(x0_stored, b * 16 + 16)
                        pool.wait_ge(node_b_stored, b * 16 + 16)
                    sum_tile(b, j)

        @block.scalar
        def _(sc):
            def adj_hi_part(blk, c, held=True):
                rounds = CHUNKS // RAW_RING
                sc.wait_ge(raw_full[c % RAW_RING], (blk * rounds + c // RAW_RING + 1) * 16)
                if held:
                    sc.wait_ge(chunk_used, blk * CHUNKS + c - RING + 1)
                nc.scalar.activation(adj_hi[:, c % RING, :], adj_raw[:, c % RAW_RING, :], ACT.Copy).then_inc(hi_ready, 1)

            def root(n, tiles=slice(0, TILES)):
                sc.wait_ge(ln_step, n * LN_STEPS + 5)
                nc.scalar.activation(std[:, tiles], var[:, tiles], ACT.Sqrt).then_inc(ln_root, 1)

            def take_act(source, br, func, **affine):
                nc.scalar.activation(act_f32[:, br, :], source, func, **affine).then_inc(act_f32_ready[br], 1)
                nc.scalar.activation(act_hi[:, br, :], source, func, **affine).then_inc(act_hi_ready[br], 1)

            def take_acc(b, br):
                if br == 0:
                    sc.wait_ge(acc_h_done, b + 1)
                else:
                    sc.wait_ge(chunk_used, (b + 1) * CHUNKS)
                take_act((acc_h, acc_x2)[br][:], br, ACT.Copy, scale=rows[:, D + br:D + br + 1])

            def mlp_relu(b, layer):
                for br in range(BRANCHES):
                    sc.wait_ge(mlp_done[br], b * LAYERS + layer + 1)
                    at = K + br * LAYERS + layer
                    take_act(mlp_acc[br][:], br, ACT.Relu, bias=small[:, at:at + 1])

            def take_turned(b):
                sc.wait_ge(turn_done, b + 1)
                nc.scalar.activation(h2t_hi[:], turned[:], ACT.Relu).then_inc(h2t_hi_ready, 1)

            def take_aux(b):
                sc.wait_ge(sum_step, (b * TILES + 1) * SUM_STEPS)
                for half in range(2):
                    got = mlp_acc[half][:, 0:2 * AUX].rearrange("p (t c) -> p t c", t=2)
                    t = slice(2 * half, 2 * half + 2)
                    sc.wait_ge(aux_done, b * 2 + half + 1)
                    nc.scalar.activation(node_b_new[:, t, :], got[:, :, 0:D], ACT.Copy)
                    nc.scalar.activation(node[:, t, :], got[:, :, D:AUX], ACT.Copy).then_inc(node_ready, 1)

            def node_work(b, at):
                return plan([(LAG - 1, lambda: take_acc(b, 0)), (LAG - 1, lambda: take_acc(b, 1))]
                            + [(LAG + at["mlp"][n], lambda n=n: mlp_relu(b, n)) for n in range(LAYERS)]
                            + [(LAG + at["merge"] + 1, lambda: root(b + len(BATCHES))),
                               (LAG + at["turn"], lambda: take_turned(b)),
                               (LAG + at["aux"], lambda: take_aux(b))])

            sc.wait_ge(consts, 3)
            nc.scalar.activation(spare[:, 0:1], ln_eps[:], ACT.Sqrt)

            def x2_hi_part(g):
                sc.wait_ge(x2_in[g % QUARTERS], (g // QUARTERS + 1) * 16)
                nc.scalar.activation(x2_hi[:, tiles_of(g), :],
                                     x2_raw[:, g % QUARTERS, :].rearrange("p (t d) -> p t d", t=TILES),
                                     ACT.Copy).then_inc(x2_hi_ready, 1)

            def h_hi_part(g):
                sc.wait_ge(normed_ready, g + 1)
                nc.scalar.activation(h_hi[:, tiles_of(g), :], normed[:], ACT.Relu).then_inc(h_hi_ready, 1)

            def square_hi_part():
                sc.wait_ge(square_in, 16)
                nc.scalar.activation(square_hi[:], act_f32[:].rearrange("p b n -> p (b n)"),
                                     ACT.Copy).then_inc(square_hi_ready, 1)

            def aux_hi_part():
                sc.wait_ge(small_in, 16)
                nc.scalar.activation(aux_hi[:, D:AUX], small[:, 0:K], ACT.Copy).then_inc(aux_hi_ready, 1)
                sc.wait_ge(w1b_done, 1)
                nc.scalar.activation(aux_hi[:, 0:D], bank[2][:, 0:D], ACT.Copy).then_inc(aux_hi_ready, 1)

            work = plan([(0, lambda: root(0, batch_tiles(0))), (0, lambda: x2_hi_part(0)),
                         (1, lambda: h_hi_part(0)), (2, lambda: x2_hi_part(1)), (2, lambda: h_hi_part(1)),
                         (3, lambda: x2_hi_part(2)), (4, lambda: root(1, batch_tiles(1))),
                         (4, lambda: h_hi_part(2)), (5, lambda: x2_hi_part(3)), (5, lambda: h_hi_part(3)),
                         (6, lambda: x2_hi_part(4)), (7, lambda: root(2, batch_tiles(2))),
                         (8, lambda: h_hi_part(4)), (8, lambda: x2_hi_part(5)), (9, lambda: h_hi_part(5)),
                         (10, lambda: x2_hi_part(6)), (11, lambda: h_hi_part(6)), (12, lambda: x2_hi_part(7)),
                         (12, square_hi_part), (13, lambda: h_hi_part(7)), (14, aux_hi_part)])
            for c in range(CHUNKS):
                adj_hi_part(0, c, held=c >= RING)
                for step in work.get(c, []):
                    step()
            sc.wait_ge(scale_ready, 1)
            sc.wait_ge(square_lo_ready, 1)

            def pair_hi_part():
                sc.wait_ge(pair_in, 16)
                for n in range(QUARTERS):
                    nc.scalar.activation(pair_hi[:, n * BLOCK:(n + 1) * BLOCK],
                                         prod[:, n, :, :].rearrange("p k f -> p (k f)"),
                                         ACT.Copy).then_inc(pair_hi_ready, 1)

            pair_hi_part()

            with sc.Fori(0, BLOCKS - 1) as b:
                work = node_work(b, FIRST_PASS)
                for c in range(CHUNKS):
                    adj_hi_part(b + 1, c)
                    for step in work.get(c, []):
                        step()

            def y_hi_part(g):
                sc.wait_ge(sum_step, (g * TILES + TILES + 1) * SUM_STEPS)
                sc.wait_ge(chunk_used, (BLOCKS - 1) * CHUNKS + (g + 1) * TILES // PER_CHUNK)
                nc.scalar.activation(y_hi[:, tiles_of(g), :], y[:, tiles_of(g), :], ACT.Copy).then_inc(y_hi_ready, 1)

            def take_accy(b, parity, chunks):
                sc.wait_ge(chunk_used, chunks)
                nc.scalar.activation(act_f32[:, parity, :], acc_y[parity][:], ACT.Copy).then_inc(accy_out, 1)

            work = node_work(BLOCKS - 1, SECOND_PASS)
            for at in range(2 * CHUNKS):
                adj_hi_part(BLOCKS, at)
                if at in y_parts_at:
                    y_hi_part(y_parts_at.index(at))
                for step in work.get(at, []):
                    step()
                if at == 2 * CHUNKS - 1:
                    take_accy(0, 0, BLOCKS * CHUNKS + END_OF_0 + 1)

            def second_pass_block(b, parity):
                for c in range(CHUNKS):
                    adj_hi_part(b + BLOCKS, c)
                    if c == LAG - 1:
                        take_accy(b - 1, 1 - parity, (b + BLOCKS) * CHUNKS)

            with sc.Fori(0, PAIRS - 1) as pair:
                second_pass_block(pair * 2 + 2, 0)
                second_pass_block(pair * 2 + 3, 1)
            take_accy(BLOCKS - 1, 1, 2 * BLOCKS * CHUNKS)

        @block.vector
        def _(ve):
            def adj_lo_part(blk, c, held=True):
                ve.wait_ge(hi_ready, blk * CHUNKS + c + 1)
                if held:
                    ve.wait_ge(chunk_used, blk * CHUNKS + c - RING + 1)
                nc.vector.tensor_tensor(adj_lo[:, c % RING, :], adj_raw[:, c % RAW_RING, :],
                                        adj_hi[:, c % RING, :].bitcast(F32), ALU.subtract).then_inc(lo_ready, 1)

            def row_halves(rows, tiles):
                for j in range(tiles.start, tiles.stop):
                    done = nc.vector.bn_stats(halves[:, j, :], rows[:, j, :])
                return done

            def row_moments(n, tiles):
                at = n * LN_STEPS
                ve.wait_ge(ln_step, at + 1)
                halves_t = halves[:, tiles, :]
                nc.vector.tensor_tensor(mean[:, tiles], halves_t[:, :, 1], halves_t[:, :, 4], ALU.add)
                nc.vector.tensor_tensor(mean_gap[:, tiles], halves_t[:, :, 1], halves_t[:, :, 4], ALU.subtract)
                nc.vector.tensor_tensor(squares[:, tiles], halves_t[:, :, 2], halves_t[:, :, 5],
                                        ALU.add).then_inc(ln_step, 1)
                ve.wait_ge(ln_step, at + 2)
                nc.vector.tensor_scalar(mean[:, tiles], mean[:, tiles], 0.5, None, ALU.mult)
                nc.vector.scalar_tensor_tensor(mean_gap[:, tiles], mean_gap[:, tiles], 0.25, mean_gap[:, tiles],
                                               ALU.mult, ALU.mult).then_inc(ln_step, 1)
                ve.wait_ge(ln_step, at + 3)
                nc.vector.scalar_tensor_tensor(squares[:, tiles], squares[:, tiles], 1.0 / D, mean_gap[:, tiles],
                                               ALU.mult, ALU.add).then_inc(ln_step, 1)
                ve.wait_ge(ln_step, at + 4)
                nc.vector.tensor_scalar(var[:, tiles], squares[:, tiles], LN_EPS, None, ALU.add).then_inc(ln_step, 1)

            def row_scale(n, tiles):
                at = n * LN_STEPS + 5
                r, t = rstd[:, tiles], newton[:, tiles]
                ve.wait_ge(ln_root, n + 1)
                nc.vector.reciprocal(r, std[:, tiles]).then_inc(ln_step, 1)
                ve.wait_ge(ln_step, at + 1)
                nc.vector.tensor_tensor(t, r, r, ALU.mult).then_inc(ln_step, 1)
                ve.wait_ge(ln_step, at + 2)
                nc.vector.scalar_tensor_tensor(t, t, -0.5, var[:, tiles], ALU.mult, ALU.mult).then_inc(ln_step, 1)
                ve.wait_ge(ln_step, at + 3)
                nc.vector.scalar_tensor_tensor(r, t, 1.5, r, ALU.add, ALU.mult).then_inc(ln_step, 1)
                ve.wait_ge(ln_step, at + 4)

            def normalize(rows, tiles):
                for j in range(TILES):
                    col = slice(tiles.start + j, tiles.start + j + 1)
                    done = nc.vector.tensor_scalar(normed[:, j, :], rows[:, tiles.start + j, :], mean[:, col],
                                                   rstd[:, col], ALU.subtract, ALU.mult)
                done.then_inc(normed_ready, 1)

            def act_lo_part(b, n):
                for br in range(BRANCHES):
                    ve.wait_ge(act_f32_ready[br], b * (LAYERS + 1) + n + 1)
                    ve.wait_ge(act_hi_ready[br], b * (LAYERS + 1) + n + 1)
                    nc.vector.tensor_tensor(act_lo[:, br, :], act_f32[:, br, :], act_hi[:, br, :].bitcast(F32),
                                            ALU.subtract).then_inc(act_lo_ready[br], 1)

            def add_residual(b):
                ve.wait_ge(merge_done, b + 1)
                ve.wait_ge(sum_step, (b * TILES + 1) * SUM_STEPS)
                nc.vector.tensor_tensor(x0_new[:], merged[:].rearrange("p (t d) -> p t d", t=TILES),
                                        y[:, bass.ds(b * TILES, TILES), :], ALU.add).then_inc(x0_ready, 1)
                ve.wait_ge(x0_ready, b + 1)
                row_halves(x0_new[:], slice(0, TILES)).then_inc(ln_step, 1)
                row_moments(b + len(BATCHES), slice(0, TILES))

            def scale_x0(b):
                row_scale(b + len(BATCHES), slice(0, TILES))
                normalize(x0_new[:], slice(0, TILES))

            def h2t_lo_part(b):
                ve.wait_ge(h2t_hi_ready, b + 1)
                nc.vector.scalar_tensor_tensor(h2t_lo[:], turned[:], 0.0, h2t_hi[:].bitcast(F32), ALU.max,
                                               ALU.subtract).then_inc(h2t_lo_ready, 1)

            def weigh(b, n):
                j, q = n // QUARTERS, n % QUARTERS
                ve.wait_ge(pair_done, b * BANKS + n + 1)
                ve.wait_ge(node_ready, b * 2 + j // 2 + 1)
                ve.wait_ge(sum_step, (b * TILES + j) * SUM_STEPS + max(q, 1))
                coef = node[:, j, q * QK:(q + 1) * QK].rearrange("p (k o) -> p k o", o=1).to_broadcast([P, QK, D])
                nc.vector.tensor_tensor(prod[:, q], pair_acc[q][:].rearrange("p (k f) -> p k f", k=QK), coef,
                                        ALU.mult).then_inc(prod_done, 1)

            def node_work(b, at, end):
                return plan([(LAG, lambda: act_lo_part(b, 0))]
                            + [(LAG + at["mlp"][n], lambda n=n: act_lo_part(b, n + 1)) for n in range(LAYERS)]
                            + [(LAG + at["merge"], lambda: add_residual(b)),
                               (LAG + at["merge"] + 2, lambda: scale_x0(b)),
                               (LAG + at["turn"], lambda: h2t_lo_part(b))]
                            + [(min(LAG + at["pair"](n), end), lambda n=n: weigh(b, n)) for n in range(BANKS)])

            nc.vector.memset(spare[:, 1:2], 0.0).then_inc(prod_done, 1)
            nc.vector.memset(spare[:, 2:3], 0.0).then_inc(out_ready, 1)
            for parity in range(2):
                nc.vector.memset(spare[:, 3 + parity:4 + parity], 0.0).then_inc(out_stored[parity], 16)

            def x_halves(g):
                ve.wait_ge(x_in[g], 16)
                done = row_halves(y[:], tiles_of(g))
                if any(g == groups[-1] for groups in BATCHES):
                    done.then_inc(ln_step, 1)

            def x_moments(n):
                row_moments(n, batch_tiles(n))

            def x_scale(n):
                row_scale(n, batch_tiles(n))

            def normalize_x(g):
                if g > 0:
                    ve.wait_ge(h_lo_ready, g)
                normalize(y[:], tiles_of(g))

            def h_lo_part(g):
                ve.wait_ge(h_hi_ready, g + 1)
                nc.vector.scalar_tensor_tensor(h_lo[:, tiles_of(g), :], normed[:], 0.0,
                                               h_hi[:, tiles_of(g), :].bitcast(F32), ALU.max,
                                               ALU.subtract).then_inc(h_lo_ready, 1)

            def eps_plus_2():
                ve.wait_ge(rows_in, 16)
                nc.vector.tensor_scalar(rows[:, D:D + BRANCHES], rows[:, D:D + BRANCHES], 2.0, None,
                                        ALU.add).then_inc(scale_ready, 1)

            def square_lo_part():
                ve.wait_ge(square_hi_ready, 1)
                nc.vector.tensor_tensor(square_lo[:], act_f32[:].rearrange("p b n -> p (b n)"),
                                        square_hi[:].bitcast(F32), ALU.subtract).then_inc(square_lo_ready, 1)

            def aux_lo_part():
                ve.wait_ge(aux_hi_ready, 2)
                nc.vector.tensor_tensor(aux_lo[:, D:AUX], small[:, 0:K], aux_hi[:, D:AUX].bitcast(F32), ALU.subtract)
                nc.vector.tensor_tensor(aux_lo[:, 0:D], bank[2][:, 0:D], aux_hi[:, 0:D].bitcast(F32),
                                        ALU.subtract).then_inc(aux_lo_ready, 1)

            work = plan([(0, lambda: x_scale(0)), (0, lambda: normalize_x(0)),
                         (1, lambda: h_lo_part(0)), (1, lambda: normalize_x(1)),
                         (2, lambda: h_lo_part(1)),
                         (3, lambda: x_halves(2)), (3, lambda: x_halves(3)), (3, lambda: x_moments(1)),
                         (3, lambda: x_scale(1)), (3, lambda: normalize_x(2)), (3, lambda: h_lo_part(2)),
                         (4, lambda: normalize_x(3)), (4, lambda: x_halves(4)),
                         (5, lambda: h_lo_part(3)), (5, lambda: x_halves(5)),
                         (6, lambda: x_halves(6)), (6, lambda: x_halves(7)), (6, lambda: x_moments(2)),
                         (7, lambda: x_scale(2)), (7, lambda: normalize_x(4)),
                         (8, lambda: h_lo_part(4)), (8, lambda: normalize_x(5)),
                         (9, lambda: h_lo_part(5)), (9, eps_plus_2), (10, lambda: normalize_x(6)),
                         (11, lambda: h_lo_part(6)), (12, lambda: normalize_x(7)),
                         (13, lambda: h_lo_part(7)), (14, square_lo_part), (15, aux_lo_part)])
            x_halves(0)
            x_halves(1)
            x_moments(0)
            for c in range(CHUNKS):
                adj_lo_part(0, c, held=c >= RING)
                for step in work.get(c, []):
                    step()
            ve.wait_ge(bm_added, BLOCKS)

            with ve.Fori(0, BLOCKS - 1) as b:
                work = node_work(b, FIRST_PASS, CHUNKS - 1)
                for c in range(CHUNKS):
                    adj_lo_part(b + 1, c)
                    for step in work.get(c, []):
                        step()

            def y_lo_part(g):
                ve.wait_ge(y_hi_ready, g + 1)
                nc.vector.tensor_tensor(y_lo[:, tiles_of(g), :], y[:, tiles_of(g), :],
                                        y_hi[:, tiles_of(g), :].bitcast(F32), ALU.subtract).then_inc(y_lo_ready, 1)

            def finish(b, parity):
                t = bass.ds(b * TILES, TILES)
                ve.wait_ge(back_done, b + 1)
                ve.wait_ge(out_ready, b + 1)
                nc.vector.tensor_tensor(biased_y[:], out_acc[parity][:].rearrange("p (t d) -> p t d", t=TILES),
                                        node_b[:, t, :], ALU.add).then_inc(biased, 1)
                ve.wait_ge(biased, b + 1)
                ve.wait_ge(out_stored[parity], (b - parity) * 8 + 16)
                nc.vector.scalar_tensor_tensor(out_buf[parity][:], biased_y[:], 0.0, x0[:, t, :], ALU.max,
                                               ALU.add).then_inc(out_ready, 1)

            work = node_work(BLOCKS - 1, SECOND_PASS, 2 * CHUNKS - 1)
            for at in range(2 * CHUNKS):
                adj_lo_part(BLOCKS, at)
                if at in y_parts_at:
                    y_lo_part(y_parts_at.index(at))
                for step in work.get(at, []):
                    step()
            ve.wait_ge(kept_in, 32 * BLOCKS)

            def second_pass_block(b, parity):
                for c in range(CHUNKS):
                    adj_lo_part(b + BLOCKS, c)
                    if c == 1:
                        finish(b - 2, parity)

            with ve.Fori(0, PAIRS - 1) as pair:
                second_pass_block(pair * 2 + 2, 0)
                second_pass_block(pair * 2 + 3, 1)
            finish(BLOCKS - 2, 0)
            finish(BLOCKS - 1, 1)

        @block.tensor
        def _(pe):
            def exact(acc, hi, lo, right_hi, right_lo, start, stop):
                nc.tensor.matmul(acc, hi, right_hi, start=start, stop=False)
                nc.tensor.matmul(acc, hi, right_lo, start=False, stop=False)
                return nc.tensor.matmul(acc, lo, right_hi, start=False, stop=stop)

            def times_adj(acc, hi, lo, c, slot):
                for n in range(PER_CHUNK):
                    k = c * PER_CHUNK + n
                    cols = slice(n * BLOCK, (n + 1) * BLOCK)
                    done = exact(acc[:], hi[:, k, :], lo[:, k, :], adj_hi[:, slot, cols], adj_lo[:, slot, cols],
                                 start=(k == 0), stop=(k == NODE_TILES - 1))
                return done

            def first_pass_chunk(blk, c, before=None):
                pe.wait_ge(lo_ready, blk * CHUNKS + c + 1)
                if c == 0 and before is not None:
                    pe.wait_ge(act_hi_ready[0], before * (LAYERS + 1) + 1)
                done = times_adj(acc_h, h_hi, h_lo, c, c % RING)
                if c == CHUNKS - 1:
                    done.then_inc(acc_h_done, 1)
                if c == 0 and before is not None:
                    pe.wait_ge(act_hi_ready[1], before * (LAYERS + 1) + 1)
                times_adj(acc_x2, x2_hi, x2_lo, c, c % RING).then_inc(chunk_used, 1)

            def first_block_x2(c):
                pe.wait_ge(lo_ready, c + 1)
                if c % 2 == 0:
                    pe.wait_ge(x2_lo_ready, c // 2 + 1)
                times_adj(acc_x2, x2_hi, x2_lo, c, c % RING)

            def first_block_h(c):
                if c % 2 == 0:
                    pe.wait_ge(h_lo_ready, c // 2 + 1)
                done = times_adj(acc_h, h_hi, h_lo, c, c % RING)
                done.then_inc(chunk_used, 1)

            def mlp_layer(b, layer):
                for br in range(BRANCHES):
                    w = slice((br * LAYERS + layer) * D, (br * LAYERS + layer + 1) * D)
                    pe.wait_ge(act_lo_ready[br], b * (LAYERS + 1) + layer + 1)
                    exact(mlp_acc[br][:], square_hi[:, w], square_lo[:, w], act_hi[:, br, :], act_lo[:, br, :],
                          start=True, stop=True).then_inc(mlp_done[br], 1)

            def merge(b):
                for br in range(BRANCHES):
                    pe.wait_ge(act_lo_ready[br], (b + 1) * (LAYERS + 1))
                pe.wait_ge(prod_done, b * BANKS + 1)
                for j in range(TILES):
                    cols = slice(j * P, (j + 1) * P)
                    for br in range(BRANCHES):
                        w = slice(MERGE + br * D, MERGE + (br + 1) * D)
                        done = exact(merged[:, cols], act_hi[:, br, cols], act_lo[:, br, cols], square_hi[:, w],
                                     square_lo[:, w], start=(br == 0), stop=(br == BRANCHES - 1))
                done.then_inc(merge_done, 1)

            def turn(b):
                pe.wait_ge(normed_ready, b + BLOCKS + 1)
                for j in range(TILES):
                    done = nc.tensor.transpose(turned[:, j * P:(j + 1) * P], normed[:, j, :], ident[:])
                done.then_inc(turn_done, 1)

            def aux(b):
                pe.wait_ge(h2t_lo_ready, b + 1)
                for j in range(TILES):
                    at = (j % 2) * AUX
                    cols = slice(j * P, (j + 1) * P)
                    done = exact(mlp_acc[j // 2][:, at:at + AUX], h2t_hi[:, cols], h2t_lo[:, cols], aux_hi[:],
                                 aux_lo[:], start=True, stop=True)
                    if j % 2 == 1:
                        done.then_inc(aux_done, 1)

            def pair_bank(b, n):
                j, q = n // QUARTERS, n % QUARTERS
                cols, part = slice(j * P, (j + 1) * P), slice(q * BLOCK, (q + 1) * BLOCK)
                if n >= QUARTERS:
                    pe.wait_ge(prod_done, b * BANKS + n - QUARTERS + 2)
                exact(pair_acc[q][:], h2t_hi[:, cols], h2t_lo[:, cols], pair_hi[:, part], pair_lo[:, part],
                      start=True, stop=True).then_inc(pair_done, 1)

            def node_work(b, at):
                return plan([(at["mlp"][n], lambda n=n: mlp_layer(b, n)) for n in range(LAYERS)]
                            + [(at["merge"], lambda: merge(b)),
                               (at["turn"], lambda: turn(b)),
                               (at["aux"], lambda: aux(b))]
                            + [(at["pair"](n), lambda n=n: pair_bank(b, n)) for n in range(BANKS)])

            first_block_x2(0)
            first_block_x2(1)
            first_block_h(0)
            first_block_h(1)
            for c in range(2, CHUNKS - 1):
                first_block_x2(c)
                first_block_h(c)
                if c == 6:
                    pe.wait_ge(basis_in, 16)
                    nc.tensor.matmul(bank[2][:, 0:D], basis[:, D:D + P], basis[:, 0:D], start=True,
                                     stop=True).then_inc(w1b_done, 1)
            first_pass_chunk(0, CHUNKS - 1)
            pe.wait_ge(square_lo_ready, 1)
            pe.wait_ge(aux_lo_ready, 1)
            with pe.Fori(0, BLOCKS - 1) as b:
                work = node_work(b, FIRST_PASS)
                for c in range(CHUNKS):
                    first_pass_chunk(b + 1, c, before=b)
                    if c == FIRST_PASS["pair"](0):
                        pe.wait_ge(pair_lo_ready, QUARTERS)
                    for step in work.get(c, []):
                        step()

            def second_pass_chunk(parity, c, at, used):
                pe.wait_ge(lo_ready, used + 1)
                times_adj(acc_y[parity], y_hi, y_lo, c, at % RING).then_inc(chunk_used, 1)

            def turn_back(b, parity):
                pe.wait_ge(accy_out, b + 1)
                pe.wait_ge(out_ready, b - parity + 1)
                for j in range(TILES):
                    cols = slice(j * P, (j + 1) * P)
                    done = nc.tensor.transpose(out_acc[parity][:, cols], act_f32[:, parity, cols], ident[:])
                done.then_inc(back_done, 1)

            work = node_work(BLOCKS - 1, SECOND_PASS)
            for at, (b, c) in enumerate(opening):
                if c % 2 == 0:
                    pe.wait_ge(y_lo_ready, c // 2 + 1)
                if c == 0:
                    pe.wait_ge(act_hi_ready[b], (BLOCKS - 1) * (LAYERS + 1) + 1)
                second_pass_chunk(b, c, at, BLOCKS * CHUNKS + at)
                for step in work.get(at, []):
                    step()
            turn_back(0, 0)

            def second_pass_block(b, parity):
                for c in range(CHUNKS):
                    second_pass_chunk(parity, c, c, (b + BLOCKS) * CHUNKS + c)
                    if c == 1:
                        turn_back(b - 1, 1 - parity)

            with pe.Fori(0, PAIRS - 1) as pair:
                second_pass_block(pair * 2 + 2, 0)
                second_pass_block(pair * 2 + 3, 1)
            turn_back(BLOCKS - 1, 1)


def kernel(**inputs):
    import numpy as np
    import concourse.bacc as bacc
    from concourse.bass_utils import run_bass_kernel_spmd

    def plain(a):
        return np.ascontiguousarray(a)

    adj = np.asarray(inputs["adj"])
    n = adj.shape[0]
    blocks, chunks = n // BLOCK, n // (P * PER_CHUNK)
    adj_t = adj.reshape(blocks, BLOCK, chunks, PER_CHUNK, P).transpose(0, 2, 4, 3, 1)
    w1, w2 = np.asarray(inputs["L0_gnn_W1"]), np.asarray(inputs["L0_gnn_W2"])
    wm = np.asarray(inputs["L0_gnn_Wm"])
    node_w = np.asarray(inputs["L1_gnn_W1"])
    arrays = {
        "x": plain(inputs["x"]),
        "adj_t": plain(adj_t).reshape(blocks, chunks, P, PER_CHUNK * BLOCK),
        "x2": plain(inputs["L0_gnn_x2"]),
        "square_w": plain(np.concatenate([w1.transpose(2, 0, 1).reshape(D, -1), w2.transpose(2, 0, 1).reshape(D, -1),
                                          wm[:, :D].T, wm[:, D:].T], axis=1)),
        "small_w": plain(np.concatenate([node_w, np.asarray(inputs["L0_gnn_b1"]).T,
                                         np.asarray(inputs["L0_gnn_b2"]).T], axis=1)),
        "basis_w": plain(np.concatenate([np.asarray(inputs["L1_gnn_b"]), node_w.T], axis=1)),
        "row_w": plain(np.concatenate([np.asarray(inputs["L0_gnn_bm"]), np.asarray(inputs["L0_gnn_eps1"]),
                                       np.asarray(inputs["L0_gnn_eps2"])])),
        "pair_w": plain(np.asarray(inputs["L1_gnn_W2"]).transpose(1, 0, 2)).reshape(D, -1),
    }
    nc = bacc.Bacc("TRN2", target_bir_lowering=False, num_devices=1)
    args = [nc.dram_tensor(name, a.shape, mybir.dt.from_np(a.dtype), kind="ExternalInput").ap()
            for name, a in arrays.items()]
    out = nc.dram_tensor("out", (n, D), F32, kind="ExternalOutput").ap()
    two_layer_graph_kernel(nc, *args, out)
    result = run_bass_kernel_spmd(nc, [arrays], core_ids=[0])
    return result.results[0]["out"]
```

```python
from contextlib import ExitStack

import concourse.bass as bass
from concourse import mybir

F32 = mybir.dt.float32
F32R = mybir.dt.float32r
ALU = mybir.AluOpType
ACT = mybir.ActivationFunctionType

P = 128
D = 128
BLOCK = 512
TILES = BLOCK // P
PER_CHUNK = 2
RAW_RING = 8
RING = 4
LAG = 3
LAYERS = 3
BRANCHES = 2
LN_EPS = 1e-5
LN_STEPS = 9

FIRST_PASS = {"mlp": (1, 2, 3), "merge": 5, "turn": 8, "aux": 10, "pair": lambda n: 11 + n // 4}
SECOND_PASS = {"mlp": (2, 4, 6), "merge": 8, "turn": 12, "aux": 14, "pair": lambda n: 15 + n // 2}


def plan(steps):
    by_chunk = {}
    for chunk, step in steps:
        by_chunk.setdefault(chunk, []).append(step)
    return by_chunk


def two_layer_graph_kernel(nc, x, adj_t, x2, square_w, small_w, basis_w, row_w, pair_w, out):
    N = x.shape[0]
    NODE_TILES = N // P
    BLOCKS = N // BLOCK
    CHUNKS = NODE_TILES // PER_CHUNK
    K = basis_w.shape[0]
    QK = BLOCK // D
    QUARTERS = K // QK
    BANKS = TILES * QUARTERS
    AUX = D + K
    PAIRS = BLOCKS // 2
    MERGE = BRANCHES * LAYERS * D
    SUM_STEPS = QUARTERS + 1

    LATE = CHUNKS - BLOCK // P // PER_CHUNK
    opening = ([(0, c) for c in range(LATE)] + [(1, c) for c in range(LATE)]
               + [(b, c) for c in range(LATE, CHUNKS) for b in range(2)])
    END_OF_0 = opening.index((0, CHUNKS - 1))
    kept_at = [0, 0] + [2 * g - 3 for g in range(2, BLOCKS - 1)] + [2 * LATE]
    MORE_SLOTS_AT = SECOND_PASS["merge"] + LAG + RAW_RING
    y_pieces = ([slice(g * TILES, (g + 1) * TILES) for g in range(BLOCKS - 1)]
                + [slice(c * PER_CHUNK, (c + 1) * PER_CHUNK) for c in range(LATE, CHUNKS)])
    y_pieces_at = [0, 1] + [2 * g - 1 for g in range(2, BLOCKS - 1)] + [2 * LATE, 2 * LATE + 2]
    pool_pieces = range(2, BLOCKS - 1)
    vector_pieces = [n for n in range(len(y_pieces)) if n not in pool_pieces]

    x_tiles = x.rearrange("(t p) d -> p t d", p=P)
    x2_tiles = x2.rearrange("(t p) d -> p t d", p=P)
    out_tiles = out.rearrange("(b t p) d -> b p t d", p=P, t=TILES)
    x0_dram = nc.dram_tensor("x0_kept", (P, NODE_TILES, D), F32, kind="Internal").ap()
    node_b_dram = nc.dram_tensor("node_b_kept", (P, NODE_TILES, D), F32, kind="Internal").ap()

    BATCHES = (range(0, 2), range(2, 4), range(4, BLOCKS))
    BATCH_OF = [n for n, groups in enumerate(BATCHES) for _ in groups]

    def batch_tiles(n):
        return slice(BATCHES[n][0] * TILES, (BATCHES[n][-1] + 1) * TILES)

    def tiles_of(g):
        return slice(g * TILES, (g + 1) * TILES)

    with ExitStack() as ctx:
        def sb(name, shape, dt=F32, within=ctx):
            return within.enter_context(nc.sbuf_tensor(name, shape, dt))

        def sem(name):
            return ctx.enter_context(nc.semaphore(name))

        adj_raw = sb("adj_raw", [P, RAW_RING, PER_CHUNK * BLOCK])
        adj_hi = sb("adj_hi", [P, RING, PER_CHUNK * BLOCK], F32R)
        adj_lo = sb("adj_lo", [P, RING, PER_CHUNK * BLOCK], F32R)
        h_hi = sb("h_hi", [P, NODE_TILES, D], F32R)
        h_lo = sb("h_lo", [P, NODE_TILES, D], F32R)
        y_hi, y_lo = h_hi, h_lo
        y = sb("y", [P, NODE_TILES, D])
        aux_hi = sb("aux_hi", [P, AUX], F32R)
        aux_lo = sb("aux_lo", [P, AUX], F32R)
        small = sb("small", [P, K + BRANCHES * LAYERS])
        basis = sb("basis", [K, D + P])
        rows = sb("rows", [P, D + BRANCHES])
        ident = sb("ident", [P, P])
        ln_eps = sb("ln_eps", [P, 1])
        act_f32 = sb("act_f32", [P, BRANCHES, BLOCK])
        x0_new = sb("x0_new", [P, TILES, D])
        normed = sb("normed", [P, TILES, D])
        node_b_new = sb("node_b_new", [P, TILES, D])
        h2t_hi = sb("h2t_hi", [P, BLOCK], F32R)
        h2t_lo = sb("h2t_lo", [P, BLOCK], F32R)
        node = sb("node", [P, TILES, K])
        prod = sb("prod", [P, QUARTERS, QK, D])
        psums = sb("psums", [P, QK, D])
        halves = sb("halves", [P, NODE_TILES, 6])
        stat = sb("stat", [P, 8, NODE_TILES])
        var, std, rstd, newton, mean, mean_gap, squares, spare = (stat[:, n, :] for n in range(8))
        shift = squares
        with ExitStack() as first_pass:
            x2_hi = sb("x2_hi", [P, NODE_TILES, D], F32R, first_pass)
            x2_lo = sb("x2_lo", [P, NODE_TILES, D], F32R, first_pass)
            square_hi = sb("square_hi", [P, MERGE + BRANCHES * D], F32R, first_pass)
            square_lo = sb("square_lo", [P, MERGE + BRANCHES * D], F32R, first_pass)
            act_hi = sb("act_hi", [P, BRANCHES, BLOCK], F32R, first_pass)
            act_lo = sb("act_lo", [P, BRANCHES, BLOCK], F32R, first_pass)
            pair_hi = sb("pair_hi", [P, K * D], F32R, first_pass)
            pair_lo = sb("pair_lo", [P, K * D], F32R, first_pass)
        x0 = sb("x0", [P, NODE_TILES, D])
        node_b = sb("node_b", [P, NODE_TILES, D])
        more_raw = sb("more_raw", [P, CHUNKS - RAW_RING, PER_CHUNK * BLOCK])
        biased_y = node_b_new
        out_buf = [x0_new, normed]

        def long_ring(c):
            return adj_raw[:, c, :] if c < RAW_RING else more_raw[:, c - RAW_RING, :]

        def long_ring_count(b, c):
            rounds = BLOCKS * CHUNKS // RAW_RING + 2 * CHUNKS // RAW_RING if c < RAW_RING else 0
            return (b - 2 + rounds + 1) * 16

        x2_raw = prod[:].rearrange("p q k f -> p q (k f)")

        bank = [ctx.enter_context(nc.psum_tensor(f"bank{n}", [P, BLOCK], F32)) for n in range(8)]
        acc_h, acc_x2 = bank[0], bank[1]
        acc_y = [bank[0], bank[1]]
        mlp_acc = [bank[2], bank[3]]
        pair_acc = bank[4:8]
        merged, turned = bank[4], bank[5]
        out_acc = [bank[6], bank[7]]

        raw_full = [sem(f"raw_full{n}") for n in range(CHUNKS)]
        hi_ready = sem("hi_ready")
        lo_ready = sem("lo_ready")
        chunk_used = sem("chunk_used")
        x_in = [sem(f"x_in{g}") for g in range(BLOCKS)]
        x2_in = [sem(f"x2_in{n}") for n in range(QUARTERS)]
        square_in = sem("square_in")
        small_in = sem("small_in")
        basis_in = sem("basis_in")
        rows_in = sem("rows_in")
        pair_in = sem("pair_in")
        consts = sem("consts")
        ln_step = sem("ln_step")
        ln_root = sem("ln_root")
        normed_ready = sem("normed_ready")
        h_hi_ready = sem("h_hi_ready")
        h_lo_ready = sem("h_lo_ready")
        bm_added = sem("bm_added")
        x2_hi_ready = sem("x2_hi_ready")
        x2_lo_ready = sem("x2_lo_ready")
        shift_ready = sem("shift_ready")
        scale_ready = sem("scale_ready")
        w1b_done = sem("w1b_done")
        square_hi_ready = sem("square_hi_ready")
        square_lo_ready = sem("square_lo_ready")
        aux_hi_ready = sem("aux_hi_ready")
        aux_lo_ready = sem("aux_lo_ready")
        pair_hi_ready = sem("pair_hi_ready")
        pair_lo_ready = sem("pair_lo_ready")
        acc_h_done = sem("acc_h_done")
        act_f32_ready = [sem(f"act{n}_f32_ready") for n in range(BRANCHES)]
        act_hi_ready = [sem(f"act{n}_hi_ready") for n in range(BRANCHES)]
        act_lo_ready = [sem(f"act{n}_lo_ready") for n in range(BRANCHES)]
        mlp_done = [sem(f"mlp{n}_done") for n in range(BRANCHES)]
        merge_done = sem("merge_done")
        x0_ready = sem("x0_ready")
        x0_stored = sem("x0_stored")
        turn_done = sem("turn_done")
        h2t_hi_ready = sem("h2t_hi_ready")
        h2t_lo_ready = sem("h2t_lo_ready")
        aux_done = sem("aux_done")
        node_ready = sem("node_ready")
        node_b_stored = sem("node_b_stored")
        pair_done = sem("pair_done")
        prod_done = sem("prod_done")
        sum_step = sem("sum_step")
        y_hi_ready = sem("y_hi_ready")
        y_lo_ready = sem("y_lo_ready")
        pool_y_lo_ready = sem("pool_y_lo_ready")
        kept_in = sem("kept_in")
        accy_out = sem("accy_out")
        back_done = sem("back_done")
        biased = sem("biased")
        out_ready = sem("out_ready")
        out_stored = [sem(f"out_stored{n}") for n in range(2)]

        block = ctx.enter_context(nc.Block())

        @block.sync
        def _(sp):
            def load_chunk(b, c):
                slot = c % RAW_RING
                sp.dma_start(adj_raw[:, slot, :], adj_t[b, c]).then_inc(raw_full[slot], 16)

            def slot_free(blk, c):
                sp.wait_ge(lo_ready, blk * CHUNKS + c - RAW_RING + 1)

            def load_x(g):
                sp.dma_start(y[:, tiles_of(g), :], x_tiles[:, tiles_of(g), :]).then_inc(x_in[g], 16)

            def load_x2(g):
                if g >= QUARTERS:
                    sp.wait_ge(x2_lo_ready, g - QUARTERS + 1)
                slot = g % QUARTERS
                sp.dma_start(x2_raw[:, slot, :].rearrange("p (t d) -> p t d", t=TILES),
                             x2_tiles[:, tiles_of(g), :]).then_inc(x2_in[slot], 16)

            load_x(0)
            load_x(1)
            load_chunk(0, 0)
            load_x2(0)
            load_chunk(0, 1)
            load_chunk(0, 2)
            load_x2(1)
            load_x(2)
            load_x(3)
            load_chunk(0, 3)
            load_chunk(0, 4)
            load_x2(2)
            load_chunk(0, 5)
            load_x2(3)
            for g in range(4, BLOCKS):
                load_x(g)
            for c in range(6, CHUNKS):
                if c >= RAW_RING:
                    slot_free(0, c)
                load_chunk(0, c)
                if c % 2 == 1 and c // 2 + 1 < BLOCKS:
                    load_x2(c // 2 + 1)
            sp.wait_ge(x2_lo_ready, BLOCKS)
            sp.dma_start(prod[:].rearrange("p q k f -> p (q k f)"), pair_w).then_inc(pair_in, 16)
            with sp.Fori(0, BLOCKS - 1) as b:
                for c in range(CHUNKS):
                    slot_free(b + 1, c)
                    load_chunk(b + 1, c)

            def load_kept(g):
                tiles = tiles_of(g)
                sp.wait_ge(chunk_used, (BLOCKS - 1) * CHUNKS + (g + 1) * TILES // PER_CHUNK)
                sp.wait_ge(x0_stored, 16 * (g + 1))
                sp.dma_start(x0[:, tiles, :], x0_dram[:, tiles, :]).then_inc(kept_in, 16)
                sp.wait_ge(node_b_stored, 16 * (g + 1))
                sp.dma_start(node_b[:, tiles, :], node_b_dram[:, tiles, :]).then_inc(kept_in, 16)

            def load_long(b, c):
                sp.dma_start(long_ring(c), adj_t[b, c]).then_inc(raw_full[c], 16)

            for at, (b, c) in enumerate(opening):
                slot_free(BLOCKS, at)
                sp.dma_start(adj_raw[:, at % RAW_RING, :], adj_t[b, c]).then_inc(raw_full[at % RAW_RING], 16)
                if at == MORE_SLOTS_AT:
                    sp.wait_ge(merge_done, BLOCKS)
                    for early in range(RAW_RING, RAW_RING + 4):
                        load_long(2, early)
                for g in range(BLOCKS):
                    if kept_at[g] == at:
                        load_kept(g)

            def store(b, parity):
                sp.wait_ge(out_ready, b + 2)
                sp.dma_start(out_tiles[b], out_buf[parity][:]).then_inc(out_stored[parity], 16)

            def second_pass_block(b, parity):
                for c in range(CHUNKS):
                    sp.wait_ge(lo_ready, (b + BLOCKS - 1) * CHUNKS + c + 1)
                    load_long(b, c)
                    if c == 3:
                        store(b - 3, 1 - parity)

            for c in range(RAW_RING):
                slot_free(BLOCKS + 2, c)
                load_long(2, c)
                if c == 0:
                    sp.wait_ge(pair_done, BLOCKS * BANKS)
                if c % 2 == 1:
                    load_long(2, CHUNKS - 4 + c // 2)
            second_pass_block(3, 1)
            with sp.Fori(0, PAIRS - 2) as pair:
                second_pass_block(pair * 2 + 4, 0)
                second_pass_block(pair * 2 + 5, 1)
            store(BLOCKS - 3, 1)
            store(BLOCKS - 2, 0)
            store(BLOCKS - 1, 1)
            for parity in range(2):
                sp.wait_ge(out_stored[parity], 16 * (PAIRS + 1))

        @block.gpsimd
        def _(pool):
            nc.gpsimd.memset(ln_eps[:], LN_EPS).then_inc(consts, 1)
            nc.gpsimd.memset(ident[:], 0.0).then_inc(consts, 1)
            pool.wait_ge(consts, 2)
            nc.gpsimd.affine_select(out=ident[:], in_=ident[:], compare_op=ALU.not_equal, fill=1.0, base=0,
                                    pattern=[[-1, P]], channel_multiplier=1).then_inc(consts, 1)

            def add_bm(g):
                pool.wait_ge(normed_ready, g + 1)
                bm = rows[:, 0:D].rearrange("p (o d) -> p o d", o=1).to_broadcast([P, TILES, D])
                nc.gpsimd.tensor_tensor(y[:, tiles_of(g), :], y[:, tiles_of(g), :], bm, ALU.add).then_inc(bm_added, 1)

            for g in range(BLOCKS):
                pool.wait_ge(x2_hi_ready, g + 1)
                slot = x2_raw[:, g % QUARTERS, :].rearrange("p (t d) -> p t d", t=TILES)
                nc.gpsimd.tensor_tensor(x2_lo[:, tiles_of(g), :], slot, x2_hi[:, tiles_of(g), :].bitcast(F32),
                                        ALU.subtract).then_inc(x2_lo_ready, 1)
                if g == 0:
                    pool.dma_start(act_f32[:].rearrange("p b n -> p (b n)"), square_w).then_inc(square_in, 16)
                    pool.dma_start(small[:], small_w).then_inc(small_in, 16)
                    pool.dma_start(basis[:], basis_w).then_inc(basis_in, 16)
                    pool.dma_start(rows[:], row_w.rearrange("(o e) -> o e", o=1).to_broadcast([P, D + BRANCHES])
                                   ).then_inc(rows_in, 16)
                if g == 5:
                    pool.wait_ge(rows_in, 16)
                if g >= 5:
                    add_bm(2 * g - 10)
                    add_bm(2 * g - 9)
            add_bm(BLOCKS - 2)
            add_bm(BLOCKS - 1)
            for n in range(QUARTERS):
                cols = slice(n * BLOCK, (n + 1) * BLOCK)
                pool.wait_ge(pair_hi_ready, n + 1)
                nc.gpsimd.tensor_tensor(pair_lo[:, cols], prod[:, n, :, :].rearrange("p k f -> p (k f)"),
                                        pair_hi[:, cols].bitcast(F32), ALU.subtract).then_inc(pair_lo_ready, 1)
            nc.gpsimd.memset(psums[:, 0, 0:1], 0.0).then_inc(sum_step, SUM_STEPS)

            def keep(b):
                pool.wait_ge(x0_ready, b + 1)
                pool.wait_ge(node_ready, b * 2 + 2)
                t = bass.ds(b * TILES, TILES)
                pool.dma_start(x0_dram[:, t, :], x0_new[:]).then_inc(x0_stored, 16)
                pool.dma_start(node_b_dram[:, t, :], node_b_new[:]).then_inc(node_b_stored, 16)

            def sum_tile(b, j):
                banks = b * BANKS + j * QUARTERS + 1
                steps = (b * TILES + (j + 1)) * SUM_STEPS
                pool.wait_ge(prod_done, banks + 2)
                pool.wait_ge(sum_step, steps)
                nc.gpsimd.tensor_tensor(psums[:], prod[:, 0], prod[:, 1], ALU.add).then_inc(sum_step, 1)
                for q in range(2, QUARTERS):
                    pool.wait_ge(prod_done, banks + q + 1)
                    pool.wait_ge(sum_step, steps + q - 1)
                    nc.gpsimd.tensor_tensor(psums[:], psums[:], prod[:, q], ALU.add).then_inc(sum_step, 1)
                pool.wait_ge(sum_step, steps + QUARTERS - 1)
                nc.gpsimd.tensor_tensor(psums[:, 0:2], psums[:, 0:2], psums[:, 2:4], ALU.add).then_inc(sum_step, 1)
                pool.wait_ge(sum_step, steps + QUARTERS)
                nc.gpsimd.tensor_tensor(y[:, bass.ds(b * TILES + j, 1), :], psums[:, 0:1], psums[:, 1:2],
                                        ALU.add).then_inc(sum_step, 1)

            def keep_and_sum(b):
                keep(b)
                for j in range(TILES):
                    if j == TILES - 1:
                        pool.wait_ge(x0_stored, b * 16 + 16)
                        pool.wait_ge(node_b_stored, b * 16 + 16)
                    sum_tile(b, j)

            def y_lo_part(n):
                pool.wait_ge(y_hi_ready, n + 1)
                t = y_pieces[n]
                nc.gpsimd.tensor_tensor(y_lo[:, t, :], y[:, t, :], y_hi[:, t, :].bitcast(F32),
                                        ALU.subtract).then_inc(pool_y_lo_ready, 1)

            with pool.Fori(0, BLOCKS - 1) as b:
                keep_and_sum(b)
            for n in pool_pieces:
                y_lo_part(n)
            keep_and_sum(BLOCKS - 1)

        @block.scalar
        def _(sc):
            def adj_hi_part(blk, c, held=True):
                rounds = CHUNKS // RAW_RING
                sc.wait_ge(raw_full[c % RAW_RING], (blk * rounds + c // RAW_RING + 1) * 16)
                if held:
                    sc.wait_ge(chunk_used, blk * CHUNKS + c - RING + 1)
                nc.scalar.activation(adj_hi[:, c % RING, :], adj_raw[:, c % RAW_RING, :], ACT.Copy).then_inc(hi_ready, 1)

            def second_hi_part(b, c):
                sc.wait_ge(raw_full[c], long_ring_count(b, c))
                sc.wait_ge(chunk_used, (b + BLOCKS) * CHUNKS + c - RING + 1)
                nc.scalar.activation(adj_hi[:, c % RING, :], long_ring(c), ACT.Copy).then_inc(hi_ready, 1)

            def root(n, tiles=slice(0, TILES)):
                sc.wait_ge(ln_step, n * LN_STEPS + 5)
                nc.scalar.activation(std[:, tiles], var[:, tiles], ACT.Sqrt).then_inc(ln_root, 1)

            def take_act(source, br, func, **affine):
                nc.scalar.activation(act_f32[:, br, :], source, func, **affine).then_inc(act_f32_ready[br], 1)
                nc.scalar.activation(act_hi[:, br, :], source, func, **affine).then_inc(act_hi_ready[br], 1)

            def take_acc(b, br):
                if br == 0:
                    sc.wait_ge(acc_h_done, b + 1)
                else:
                    sc.wait_ge(chunk_used, (b + 1) * CHUNKS)
                take_act((acc_h, acc_x2)[br][:], br, ACT.Copy, scale=rows[:, D + br:D + br + 1])

            def mlp_relu(b, layer):
                for br in range(BRANCHES):
                    sc.wait_ge(mlp_done[br], b * LAYERS + layer + 1)
                    at = K + br * LAYERS + layer
                    take_act(mlp_acc[br][:], br, ACT.Relu, bias=small[:, at:at + 1])

            def take_turned(b):
                sc.wait_ge(turn_done, b + 1)
                nc.scalar.activation(h2t_hi[:], turned[:], ACT.Relu).then_inc(h2t_hi_ready, 1)

            def take_aux(b):
                sc.wait_ge(sum_step, (b * TILES + 1) * SUM_STEPS)
                for half in range(2):
                    got = mlp_acc[half][:, 0:2 * AUX].rearrange("p (t c) -> p t c", t=2)
                    t = slice(2 * half, 2 * half + 2)
                    sc.wait_ge(aux_done, b * 2 + half + 1)
                    nc.scalar.activation(node_b_new[:, t, :], got[:, :, 0:D], ACT.Copy)
                    nc.scalar.activation(node[:, t, :], got[:, :, D:AUX], ACT.Copy).then_inc(node_ready, 1)

            def node_work(b, at):
                return plan([(LAG - 1, lambda: take_acc(b, 0)), (LAG - 1, lambda: take_acc(b, 1))]
                            + [(LAG + at["mlp"][n], lambda n=n: mlp_relu(b, n)) for n in range(LAYERS)]
                            + [(LAG + at["merge"] + 1, lambda: root(b + len(BATCHES))),
                               (LAG + at["turn"], lambda: take_turned(b)),
                               (LAG + at["aux"], lambda: take_aux(b))])

            sc.wait_ge(consts, 3)
            nc.scalar.activation(spare[:, 0:1], ln_eps[:], ACT.Sqrt)

            def x2_hi_part(g):
                sc.wait_ge(x2_in[g % QUARTERS], (g // QUARTERS + 1) * 16)
                nc.scalar.activation(x2_hi[:, tiles_of(g), :],
                                     x2_raw[:, g % QUARTERS, :].rearrange("p (t d) -> p t d", t=TILES),
                                     ACT.Copy).then_inc(x2_hi_ready, 1)

            def normalize_x(g):
                sc.wait_ge(shift_ready, BATCH_OF[g] + 1)
                sc.wait_ge(h_lo_ready, g)
                for j in range(TILES):
                    col = slice(g * TILES + j, g * TILES + j + 1)
                    done = nc.scalar.activation(normed[:, j, :], y[:, g * TILES + j, :], ACT.Relu,
                                                bias=shift[:, col], scale=rstd[:, col])
                done.then_inc(normed_ready, 1)

            def h_hi_part(g):
                sc.wait_ge(normed_ready, g + 1)
                nc.scalar.activation(h_hi[:, tiles_of(g), :], normed[:], ACT.Relu).then_inc(h_hi_ready, 1)

            def square_hi_part():
                sc.wait_ge(square_in, 16)
                nc.scalar.activation(square_hi[:], act_f32[:].rearrange("p b n -> p (b n)"),
                                     ACT.Copy).then_inc(square_hi_ready, 1)

            def aux_hi_part():
                sc.wait_ge(small_in, 16)
                nc.scalar.activation(aux_hi[:, D:AUX], small[:, 0:K], ACT.Copy).then_inc(aux_hi_ready, 1)
                sc.wait_ge(w1b_done, 1)
                nc.scalar.activation(aux_hi[:, 0:D], bank[2][:, 0:D], ACT.Copy).then_inc(aux_hi_ready, 1)

            work = plan([(0, lambda: root(0, batch_tiles(0))), (0, lambda: x2_hi_part(0)),
                         (1, lambda: h_hi_part(0)),
                         (2, lambda: x2_hi_part(1)), (2, lambda: normalize_x(1)), (2, lambda: h_hi_part(1)),
                         (3, lambda: root(1, batch_tiles(1))), (3, lambda: x2_hi_part(2)),
                         (4, lambda: normalize_x(2)), (4, lambda: h_hi_part(2)),
                         (5, lambda: x2_hi_part(3)), (5, lambda: normalize_x(3)), (5, lambda: h_hi_part(3)),
                         (6, lambda: x2_hi_part(4)), (7, lambda: root(2, batch_tiles(2))),
                         (8, lambda: normalize_x(4)), (8, lambda: h_hi_part(4)),
                         (8, lambda: x2_hi_part(5)), (9, lambda: h_hi_part(5)),
                         (10, lambda: x2_hi_part(6)), (11, lambda: h_hi_part(6)),
                         (12, lambda: x2_hi_part(7)),
                         (12, square_hi_part), (13, lambda: h_hi_part(7)), (14, aux_hi_part)])
            for c in range(CHUNKS):
                adj_hi_part(0, c, held=c >= RING)
                for step in work.get(c, []):
                    step()
            sc.wait_ge(scale_ready, 1)
            sc.wait_ge(square_lo_ready, 1)

            def pair_hi_part():
                sc.wait_ge(pair_in, 16)
                for n in range(QUARTERS):
                    nc.scalar.activation(pair_hi[:, n * BLOCK:(n + 1) * BLOCK],
                                         prod[:, n, :, :].rearrange("p k f -> p (k f)"),
                                         ACT.Copy).then_inc(pair_hi_ready, 1)

            pair_hi_part()

            with sc.Fori(0, BLOCKS - 1) as b:
                work = node_work(b, FIRST_PASS)
                for c in range(CHUNKS):
                    adj_hi_part(b + 1, c)
                    for step in work.get(c, []):
                        step()

            def y_hi_part(n):
                t = y_pieces[n]
                sc.wait_ge(sum_step, (t.stop + 1) * SUM_STEPS)
                sc.wait_ge(chunk_used, (BLOCKS - 1) * CHUNKS + t.stop // PER_CHUNK)
                nc.scalar.activation(y_hi[:, t, :], y[:, t, :], ACT.Copy).then_inc(y_hi_ready, 1)

            def take_accy(b, parity, chunks):
                sc.wait_ge(chunk_used, chunks)
                nc.scalar.activation(act_f32[:, parity, :], acc_y[parity][:], ACT.Copy).then_inc(accy_out, 1)

            work = node_work(BLOCKS - 1, SECOND_PASS)
            for at in range(2 * CHUNKS):
                adj_hi_part(BLOCKS, at)
                if at in y_pieces_at:
                    y_hi_part(y_pieces_at.index(at))
                for step in work.get(at, []):
                    step()
                if at == 2 * CHUNKS - 1:
                    take_accy(0, 0, BLOCKS * CHUNKS + END_OF_0 + 1)

            def second_pass_block(b, parity):
                for c in range(CHUNKS):
                    second_hi_part(b, c)
                    if c == LAG - 1:
                        take_accy(b - 1, 1 - parity, (b + BLOCKS) * CHUNKS)

            with sc.Fori(0, PAIRS - 1) as pair:
                second_pass_block(pair * 2 + 2, 0)
                second_pass_block(pair * 2 + 3, 1)
            take_accy(BLOCKS - 1, 1, 2 * BLOCKS * CHUNKS)

        @block.vector
        def _(ve):
            def adj_lo_part(blk, c, held=True, raw=None):
                ve.wait_ge(hi_ready, blk * CHUNKS + c + 1)
                if held:
                    ve.wait_ge(chunk_used, blk * CHUNKS + c - RING + 1)
                nc.vector.tensor_tensor(adj_lo[:, c % RING, :], adj_raw[:, c % RAW_RING, :] if raw is None else raw,
                                        adj_hi[:, c % RING, :].bitcast(F32), ALU.subtract).then_inc(lo_ready, 1)

            def row_halves(rows, tiles):
                for j in range(tiles.start, tiles.stop):
                    done = nc.vector.bn_stats(halves[:, j, :], rows[:, j, :])
                return done

            def row_moments(n, tiles):
                at = n * LN_STEPS
                ve.wait_ge(ln_step, at + 1)
                halves_t = halves[:, tiles, :]
                nc.vector.tensor_tensor(mean[:, tiles], halves_t[:, :, 1], halves_t[:, :, 4], ALU.add)
                nc.vector.tensor_tensor(mean_gap[:, tiles], halves_t[:, :, 1], halves_t[:, :, 4], ALU.subtract)
                nc.vector.tensor_tensor(squares[:, tiles], halves_t[:, :, 2], halves_t[:, :, 5],
                                        ALU.add).then_inc(ln_step, 1)
                ve.wait_ge(ln_step, at + 2)
                nc.vector.tensor_scalar(mean[:, tiles], mean[:, tiles], 0.5, None, ALU.mult)
                nc.vector.scalar_tensor_tensor(mean_gap[:, tiles], mean_gap[:, tiles], 0.25, mean_gap[:, tiles],
                                               ALU.mult, ALU.mult).then_inc(ln_step, 1)
                ve.wait_ge(ln_step, at + 3)
                nc.vector.scalar_tensor_tensor(squares[:, tiles], squares[:, tiles], 1.0 / D, mean_gap[:, tiles],
                                               ALU.mult, ALU.add).then_inc(ln_step, 1)
                ve.wait_ge(ln_step, at + 4)
                nc.vector.tensor_scalar(var[:, tiles], squares[:, tiles], LN_EPS, None, ALU.add).then_inc(ln_step, 1)

            def row_scale(n, tiles):
                at = n * LN_STEPS + 5
                r, t = rstd[:, tiles], newton[:, tiles]
                ve.wait_ge(ln_root, n + 1)
                nc.vector.reciprocal(r, std[:, tiles]).then_inc(ln_step, 1)
                ve.wait_ge(ln_step, at + 1)
                nc.vector.tensor_tensor(t, r, r, ALU.mult).then_inc(ln_step, 1)
                ve.wait_ge(ln_step, at + 2)
                nc.vector.scalar_tensor_tensor(t, t, -0.5, var[:, tiles], ALU.mult, ALU.mult).then_inc(ln_step, 1)
                ve.wait_ge(ln_step, at + 3)
                nc.vector.scalar_tensor_tensor(r, t, 1.5, r, ALU.add, ALU.mult).then_inc(ln_step, 1)
                ve.wait_ge(ln_step, at + 4)

            def normalize(rows, tiles):
                for j in range(TILES):
                    col = slice(tiles.start + j, tiles.start + j + 1)
                    done = nc.vector.tensor_scalar(normed[:, j, :], rows[:, tiles.start + j, :], mean[:, col],
                                                   rstd[:, col], ALU.subtract, ALU.mult)
                done.then_inc(normed_ready, 1)

            def act_lo_part(b, n):
                for br in range(BRANCHES):
                    ve.wait_ge(act_f32_ready[br], b * (LAYERS + 1) + n + 1)
                    ve.wait_ge(act_hi_ready[br], b * (LAYERS + 1) + n + 1)
                    nc.vector.tensor_tensor(act_lo[:, br, :], act_f32[:, br, :], act_hi[:, br, :].bitcast(F32),
                                            ALU.subtract).then_inc(act_lo_ready[br], 1)

            def add_residual(b):
                ve.wait_ge(merge_done, b + 1)
                ve.wait_ge(sum_step, (b * TILES + 1) * SUM_STEPS)
                nc.vector.tensor_tensor(x0_new[:], merged[:].rearrange("p (t d) -> p t d", t=TILES),
                                        y[:, bass.ds(b * TILES, TILES), :], ALU.add).then_inc(x0_ready, 1)
                ve.wait_ge(x0_ready, b + 1)
                row_halves(x0_new[:], slice(0, TILES)).then_inc(ln_step, 1)
                row_moments(b + len(BATCHES), slice(0, TILES))

            def scale_x0(b):
                row_scale(b + len(BATCHES), slice(0, TILES))
                normalize(x0_new[:], slice(0, TILES))

            def h2t_lo_part(b):
                ve.wait_ge(h2t_hi_ready, b + 1)
                nc.vector.scalar_tensor_tensor(h2t_lo[:], turned[:], 0.0, h2t_hi[:].bitcast(F32), ALU.max,
                                               ALU.subtract).then_inc(h2t_lo_ready, 1)

            def weigh(b, n):
                j, q = n // QUARTERS, n % QUARTERS
                ve.wait_ge(pair_done, b * BANKS + n + 1)
                ve.wait_ge(node_ready, b * 2 + j // 2 + 1)
                ve.wait_ge(sum_step, (b * TILES + j) * SUM_STEPS + max(q, 1))
                coef = node[:, j, q * QK:(q + 1) * QK].rearrange("p (k o) -> p k o", o=1).to_broadcast([P, QK, D])
                nc.vector.tensor_tensor(prod[:, q], pair_acc[q][:].rearrange("p (k f) -> p k f", k=QK), coef,
                                        ALU.mult).then_inc(prod_done, 1)

            def node_work(b, at, end):
                return plan([(LAG, lambda: act_lo_part(b, 0))]
                            + [(LAG + at["mlp"][n], lambda n=n: act_lo_part(b, n + 1)) for n in range(LAYERS)]
                            + [(LAG + at["merge"], lambda: add_residual(b)),
                               (LAG + at["merge"] + 2, lambda: scale_x0(b)),
                               (LAG + at["turn"], lambda: h2t_lo_part(b))]
                            + [(min(LAG + at["pair"](n), end), lambda n=n: weigh(b, n)) for n in range(BANKS)])

            nc.vector.memset(spare[:, 1:2], 0.0).then_inc(prod_done, 1)
            nc.vector.memset(spare[:, 2:3], 0.0).then_inc(out_ready, 1)
            for parity in range(2):
                nc.vector.memset(spare[:, 3 + parity:4 + parity], 0.0).then_inc(out_stored[parity], 16)

            def x_halves(g):
                ve.wait_ge(x_in[g], 16)
                done = row_halves(y[:], tiles_of(g))
                if any(g == groups[-1] for groups in BATCHES):
                    done.then_inc(ln_step, 1)

            def x_moments(n):
                row_moments(n, batch_tiles(n))

            def x_scale(n):
                tiles = batch_tiles(n)
                row_scale(n, tiles)
                nc.vector.scalar_tensor_tensor(shift[:, tiles], mean[:, tiles], -1.0, rstd[:, tiles], ALU.mult,
                                               ALU.mult).then_inc(shift_ready, 1)

            def normalize_x(g):
                if g > 0:
                    ve.wait_ge(h_lo_ready, g)
                normalize(y[:], tiles_of(g))

            def h_lo_part(g):
                ve.wait_ge(h_hi_ready, g + 1)
                nc.vector.scalar_tensor_tensor(h_lo[:, tiles_of(g), :], normed[:], 0.0,
                                               h_hi[:, tiles_of(g), :].bitcast(F32), ALU.max,
                                               ALU.subtract).then_inc(h_lo_ready, 1)

            def eps_plus_2():
                ve.wait_ge(rows_in, 16)
                nc.vector.tensor_scalar(rows[:, D:D + BRANCHES], rows[:, D:D + BRANCHES], 2.0, None,
                                        ALU.add).then_inc(scale_ready, 1)

            def square_lo_part():
                ve.wait_ge(square_hi_ready, 1)
                nc.vector.tensor_tensor(square_lo[:], act_f32[:].rearrange("p b n -> p (b n)"),
                                        square_hi[:].bitcast(F32), ALU.subtract).then_inc(square_lo_ready, 1)

            def aux_lo_part():
                ve.wait_ge(aux_hi_ready, 2)
                nc.vector.tensor_tensor(aux_lo[:, D:AUX], small[:, 0:K], aux_hi[:, D:AUX].bitcast(F32), ALU.subtract)
                nc.vector.tensor_tensor(aux_lo[:, 0:D], bank[2][:, 0:D], aux_hi[:, 0:D].bitcast(F32),
                                        ALU.subtract).then_inc(aux_lo_ready, 1)

            work = plan([(0, lambda: x_scale(0)), (0, lambda: normalize_x(0)),
                         (1, lambda: h_lo_part(0)),
                         (2, lambda: x_halves(2)), (2, lambda: x_halves(3)), (2, lambda: h_lo_part(1)),
                         (2, lambda: x_moments(1)), (3, lambda: x_scale(1)),
                         (4, lambda: h_lo_part(2)), (4, lambda: x_halves(4)),
                         (5, lambda: x_halves(5)), (5, lambda: h_lo_part(3)),
                         (6, lambda: x_halves(6)), (6, lambda: x_halves(7)), (6, lambda: x_moments(2)),
                         (7, lambda: x_scale(2)), (8, lambda: h_lo_part(4)), (9, lambda: h_lo_part(5)),
                         (9, eps_plus_2), (12, lambda: normalize_x(7)), (10, lambda: normalize_x(6)), (8, lambda: normalize_x(5)), (11, lambda: h_lo_part(6)),
                         (12, square_lo_part), (13, lambda: h_lo_part(7)), (15, aux_lo_part)])
            x_halves(0)
            x_halves(1)
            x_moments(0)
            for c in range(CHUNKS):
                adj_lo_part(0, c, held=c >= RING)
                for step in work.get(c, []):
                    step()
            ve.wait_ge(bm_added, BLOCKS)

            with ve.Fori(0, BLOCKS - 1) as b:
                work = node_work(b, FIRST_PASS, CHUNKS - 1)
                for c in range(CHUNKS):
                    adj_lo_part(b + 1, c)
                    for step in work.get(c, []):
                        step()

            def y_lo_part(n):
                ve.wait_ge(y_hi_ready, n + 1)
                t = y_pieces[n]
                nc.vector.tensor_tensor(y_lo[:, t, :], y[:, t, :], y_hi[:, t, :].bitcast(F32),
                                        ALU.subtract).then_inc(y_lo_ready, 1)

            def finish(b, parity):
                t = bass.ds(b * TILES, TILES)
                ve.wait_ge(back_done, b + 1)
                ve.wait_ge(out_ready, b + 1)
                nc.vector.tensor_tensor(biased_y[:], out_acc[parity][:].rearrange("p (t d) -> p t d", t=TILES),
                                        node_b[:, t, :], ALU.add).then_inc(biased, 1)
                ve.wait_ge(biased, b + 1)
                ve.wait_ge(out_stored[parity], (b - parity) * 8 + 16)
                nc.vector.scalar_tensor_tensor(out_buf[parity][:], biased_y[:], 0.0, x0[:, t, :], ALU.max,
                                               ALU.add).then_inc(out_ready, 1)

            work = node_work(BLOCKS - 1, SECOND_PASS, 2 * CHUNKS - 1)
            for at in range(2 * CHUNKS):
                adj_lo_part(BLOCKS, at)
                if at in y_pieces_at and y_pieces_at.index(at) in vector_pieces:
                    y_lo_part(y_pieces_at.index(at))
                for step in work.get(at, []):
                    step()
            ve.wait_ge(kept_in, 32 * BLOCKS)

            def second_pass_block(b, parity):
                for c in range(CHUNKS):
                    adj_lo_part(b + BLOCKS, c, raw=long_ring(c))
                    if c == 1:
                        finish(b - 2, parity)

            with ve.Fori(0, PAIRS - 1) as pair:
                second_pass_block(pair * 2 + 2, 0)
                second_pass_block(pair * 2 + 3, 1)
            finish(BLOCKS - 2, 0)
            finish(BLOCKS - 1, 1)

        @block.tensor
        def _(pe):
            def exact(acc, hi, lo, right_hi, right_lo, start, stop):
                nc.tensor.matmul(acc, hi, right_hi, start=start, stop=False)
                nc.tensor.matmul(acc, hi, right_lo, start=False, stop=False)
                return nc.tensor.matmul(acc, lo, right_hi, start=False, stop=stop)

            def times_adj(acc, hi, lo, c, slot):
                for n in range(PER_CHUNK):
                    k = c * PER_CHUNK + n
                    cols = slice(n * BLOCK, (n + 1) * BLOCK)
                    done = exact(acc[:], hi[:, k, :], lo[:, k, :], adj_hi[:, slot, cols], adj_lo[:, slot, cols],
                                 start=(k == 0), stop=(k == NODE_TILES - 1))
                return done

            def first_pass_chunk(blk, c, before=None):
                pe.wait_ge(lo_ready, blk * CHUNKS + c + 1)
                if c == 0 and before is not None:
                    pe.wait_ge(act_hi_ready[0], before * (LAYERS + 1) + 1)
                done = times_adj(acc_h, h_hi, h_lo, c, c % RING)
                if c == CHUNKS - 1:
                    done.then_inc(acc_h_done, 1)
                if c == 0 and before is not None:
                    pe.wait_ge(act_hi_ready[1], before * (LAYERS + 1) + 1)
                times_adj(acc_x2, x2_hi, x2_lo, c, c % RING).then_inc(chunk_used, 1)

            def first_block_x2(c):
                pe.wait_ge(lo_ready, c + 1)
                if c % 2 == 0:
                    pe.wait_ge(x2_lo_ready, c // 2 + 1)
                times_adj(acc_x2, x2_hi, x2_lo, c, c % RING)

            def first_block_h(c):
                if c % 2 == 0:
                    pe.wait_ge(h_lo_ready, c // 2 + 1)
                done = times_adj(acc_h, h_hi, h_lo, c, c % RING)
                done.then_inc(chunk_used, 1)

            def mlp_layer(b, layer):
                for br in range(BRANCHES):
                    w = slice((br * LAYERS + layer) * D, (br * LAYERS + layer + 1) * D)
                    pe.wait_ge(act_hi_ready[br], b * (LAYERS + 1) + layer + 1)
                    nc.tensor.matmul(mlp_acc[br][:], square_hi[:, w], act_hi[:, br, :], start=True, stop=False)
                    nc.tensor.matmul(mlp_acc[br][:], square_lo[:, w], act_hi[:, br, :], start=False, stop=False)
                    pe.wait_ge(act_lo_ready[br], b * (LAYERS + 1) + layer + 1)
                    nc.tensor.matmul(mlp_acc[br][:], square_hi[:, w], act_lo[:, br, :], start=False,
                                     stop=True).then_inc(mlp_done[br], 1)

            def merge(b):
                for br in range(BRANCHES):
                    pe.wait_ge(act_lo_ready[br], (b + 1) * (LAYERS + 1))
                pe.wait_ge(prod_done, b * BANKS + 1)
                for j in range(TILES):
                    cols = slice(j * P, (j + 1) * P)
                    for br in range(BRANCHES):
                        w = slice(MERGE + br * D, MERGE + (br + 1) * D)
                        done = exact(merged[:, cols], act_hi[:, br, cols], act_lo[:, br, cols], square_hi[:, w],
                                     square_lo[:, w], start=(br == 0), stop=(br == BRANCHES - 1))
                done.then_inc(merge_done, 1)

            def turn(b):
                pe.wait_ge(normed_ready, b + BLOCKS + 1)
                for j in range(TILES):
                    done = nc.tensor.transpose(turned[:, j * P:(j + 1) * P], normed[:, j, :], ident[:])
                done.then_inc(turn_done, 1)

            def aux(b):
                pe.wait_ge(h2t_lo_ready, b + 1)
                for j in range(TILES):
                    at = (j % 2) * AUX
                    cols = slice(j * P, (j + 1) * P)
                    done = exact(mlp_acc[j // 2][:, at:at + AUX], h2t_hi[:, cols], h2t_lo[:, cols], aux_hi[:],
                                 aux_lo[:], start=True, stop=True)
                    if j % 2 == 1:
                        done.then_inc(aux_done, 1)

            def pair_bank(b, n):
                j, q = n // QUARTERS, n % QUARTERS
                cols, part = slice(j * P, (j + 1) * P), slice(q * BLOCK, (q + 1) * BLOCK)
                if n >= QUARTERS:
                    pe.wait_ge(prod_done, b * BANKS + n - QUARTERS + 2)
                exact(pair_acc[q][:], h2t_hi[:, cols], h2t_lo[:, cols], pair_hi[:, part], pair_lo[:, part],
                      start=True, stop=True).then_inc(pair_done, 1)

            def node_work(b, at):
                return plan([(at["mlp"][n], lambda n=n: mlp_layer(b, n)) for n in range(LAYERS)]
                            + [(at["merge"], lambda: merge(b)),
                               (at["turn"], lambda: turn(b)),
                               (at["aux"], lambda: aux(b))]
                            + [(at["pair"](n), lambda n=n: pair_bank(b, n)) for n in range(BANKS)])

            first_block_x2(0)
            first_block_x2(1)
            first_block_h(0)
            first_block_h(1)
            for c in range(2, CHUNKS - 1):
                first_block_x2(c)
                first_block_h(c)
                if c == 6:
                    pe.wait_ge(basis_in, 16)
                    nc.tensor.matmul(bank[2][:, 0:D], basis[:, D:D + P], basis[:, 0:D], start=True,
                                     stop=True).then_inc(w1b_done, 1)
            first_pass_chunk(0, CHUNKS - 1)
            pe.wait_ge(square_lo_ready, 1)
            pe.wait_ge(aux_lo_ready, 1)
            with pe.Fori(0, BLOCKS - 1) as b:
                work = node_work(b, FIRST_PASS)
                for c in range(CHUNKS):
                    first_pass_chunk(b + 1, c, before=b)
                    if c == FIRST_PASS["pair"](0):
                        pe.wait_ge(pair_lo_ready, QUARTERS)
                    for step in work.get(c, []):
                        step()

            def second_pass_chunk(parity, c, at, used):
                pe.wait_ge(lo_ready, used + 1)
                times_adj(acc_y[parity], y_hi, y_lo, c, at % RING).then_inc(chunk_used, 1)

            def turn_back(b, parity):
                pe.wait_ge(accy_out, b + 1)
                pe.wait_ge(out_ready, b - parity + 1)
                for j in range(TILES):
                    cols = slice(j * P, (j + 1) * P)
                    done = nc.tensor.transpose(out_acc[parity][:, cols], act_f32[:, parity, cols], ident[:])
                done.then_inc(back_done, 1)

            work = node_work(BLOCKS - 1, SECOND_PASS)
            for at, (b, c) in enumerate(opening):
                for n, t in enumerate(y_pieces):
                    if t.start == c * PER_CHUNK:
                        if n in pool_pieces:
                            pe.wait_ge(pool_y_lo_ready, pool_pieces.index(n) + 1)
                        else:
                            pe.wait_ge(y_lo_ready, vector_pieces.index(n) + 1)
                if c == 0:
                    pe.wait_ge(act_hi_ready[b], (BLOCKS - 1) * (LAYERS + 1) + 1)
                second_pass_chunk(b, c, at, BLOCKS * CHUNKS + at)
                for step in work.get(at, []):
                    step()
            turn_back(0, 0)

            def second_pass_block(b, parity):
                for c in range(CHUNKS):
                    second_pass_chunk(parity, c, c, (b + BLOCKS) * CHUNKS + c)
                    if c == 1:
                        turn_back(b - 1, 1 - parity)

            with pe.Fori(0, PAIRS - 1) as pair:
                second_pass_block(pair * 2 + 2, 0)
                second_pass_block(pair * 2 + 3, 1)
            turn_back(BLOCKS - 1, 1)


def kernel(**inputs):
    import numpy as np
    import concourse.bacc as bacc
    from concourse.bass_utils import run_bass_kernel_spmd

    def plain(a):
        return np.ascontiguousarray(a)

    adj = np.asarray(inputs["adj"])
    n = adj.shape[0]
    blocks, chunks = n // BLOCK, n // (P * PER_CHUNK)
    adj_t = adj.reshape(blocks, BLOCK, chunks, PER_CHUNK, P).transpose(0, 2, 4, 3, 1)
    w1, w2 = np.asarray(inputs["L0_gnn_W1"]), np.asarray(inputs["L0_gnn_W2"])
    wm = np.asarray(inputs["L0_gnn_Wm"])
    node_w = np.asarray(inputs["L1_gnn_W1"])
    arrays = {
        "x": plain(inputs["x"]),
        "adj_t": plain(adj_t).reshape(blocks, chunks, P, PER_CHUNK * BLOCK),
        "x2": plain(inputs["L0_gnn_x2"]),
        "square_w": plain(np.concatenate([w1.transpose(2, 0, 1).reshape(D, -1), w2.transpose(2, 0, 1).reshape(D, -1),
                                          wm[:, :D].T, wm[:, D:].T], axis=1)),
        "small_w": plain(np.concatenate([node_w, np.asarray(inputs["L0_gnn_b1"]).T,
                                         np.asarray(inputs["L0_gnn_b2"]).T], axis=1)),
        "basis_w": plain(np.concatenate([np.asarray(inputs["L1_gnn_b"]), node_w.T], axis=1)),
        "row_w": plain(np.concatenate([np.asarray(inputs["L0_gnn_bm"]), np.asarray(inputs["L0_gnn_eps1"]),
                                       np.asarray(inputs["L0_gnn_eps2"])])),
        "pair_w": plain(np.asarray(inputs["L1_gnn_W2"]).transpose(1, 0, 2)).reshape(D, -1),
    }
    nc = bacc.Bacc("TRN2", target_bir_lowering=False, num_devices=1)
    args = [nc.dram_tensor(name, a.shape, mybir.dt.from_np(a.dtype), kind="ExternalInput").ap()
            for name, a in arrays.items()]
    out = nc.dram_tensor("out", (n, D), F32, kind="ExternalOutput").ap()
    two_layer_graph_kernel(nc, *args, out)
    result = run_bass_kernel_spmd(nc, [arrays], core_ids=[0])
    return result.results[0]["out"]
```
